# Optimizing a Trainium2 kernel written in Bass

```python
import numpy as np
import jax
import jax.numpy as jnp

def _softmax(x, axis=-1):
    return jax.nn.softmax(x, axis=axis)

def _gelu(x):
    return jax.nn.gelu(x, approximate=True)

def _silu(x):
    return jax.nn.silu(x)

def _sigmoid(x):
    return jax.nn.sigmoid(x)

def _layernorm(x, axis=-1, eps=1e-05):
    m = jnp.mean(x, axis=axis, keepdims=True)
    v = jnp.var(x, axis=axis, keepdims=True)
    return (x - m) / jnp.sqrt(v + eps)

def _scatter_add(tgt, idx, src, axis=0):
    return tgt.at[idx].add(src)

def _segment_sum(src, seg, n):
    return jax.ops.segment_sum(src, seg, n)
kernel_name = 'mk_gnn_preln_d2_gnn_r64_d6fbbc'

def setup_inputs(seed: int=0):
    np.random.seed(seed)
    _w = jnp.asarray

    def _rec_inputs():
        import jax
        import jax.numpy as jnp
        _gk = jax.random.key(seed)
        x = 7.22e-05 + 1 * jax.random.normal(jax.random.fold_in(_gk, 1), (1024, 128), jnp.float32)
        src = jax.random.randint(jax.random.fold_in(_gk, 2), (32768,), 0, 1024, jnp.int32)
        dst = jax.random.randint(jax.random.fold_in(_gk, 3), (32768,), 0, 1024, jnp.int32)
        _o = jnp.argsort(dst, stable=True)
        src = src[_o]
        dst = dst[_o]
        edge_attr_64 = -1.52775e-05 + 0.999936 * jax.random.normal(jax.random.fold_in(_gk, 11), (32768, 64), jnp.float32)
        return (x, src, dst, edge_attr_64)
    x, src, dst, edge_attr_64 = _rec_inputs()

    def _L0_gnn_setup():
        import jax, jax.numpy as jnp
        import numpy as np
        NUM_NODES = 32
        N = 1024
        E = 8192
        D = 128
        ED = 64
        H = 256
        M = 128
        U = 256

        def _mlp3(x, W1, b1, W2, b2, W3, b3):
            h = jax.nn.relu(x @ W1 + b1)
            h = jax.nn.relu(h @ W2 + b2)
            return h @ W3 + b3
        key = jax.random.key(seed)
        ks = jax.random.split(key, 16)
        s = 0.02
        inp = {'node_states': jax.random.normal(ks[0], (N, D), jnp.float32), 'edges': jax.random.normal(ks[1], (E, ED), jnp.float32), 'vertices': jax.random.randint(ks[2], (E, 2), 0, N, jnp.int32), 'mW1': jax.random.normal(ks[3], (2 * D + ED, H), jnp.float32) * s, 'mb1': jnp.zeros((H,), jnp.float32), 'mW2': jax.random.normal(ks[4], (H, H), jnp.float32) * s, 'mb2': jnp.zeros((H,), jnp.float32), 'mW3': jax.random.normal(ks[5], (H, M), jnp.float32) * s, 'mb3': jnp.zeros((M,), jnp.float32), 'uW1': jax.random.normal(ks[6], (D + M + D, U), jnp.float32) * s, 'ub1': jnp.zeros((U,), jnp.float32), 'uW2': jax.random.normal(ks[7], (U, U), jnp.float32) * s, 'ub2': jnp.zeros((U,), jnp.float32), 'uW3': jax.random.normal(ks[8], (U, D), jnp.float32) * s, 'ub3': jnp.zeros((D,), jnp.float32)}
        return inp
    _L0_gnn_all = _L0_gnn_setup()
    _L0_gnn_in = {k: v for k, v in _L0_gnn_all.items() if k in ('mW1', 'mb1', 'mW2', 'mb2', 'mW3', 'mb3', 'uW1', 'ub1', 'uW2', 'ub2', 'uW3', 'ub3')}
    del _L0_gnn_all

    def _L1_gnn_setup():
        import jax, jax.numpy as jnp
        import numpy as np
        N_NODES = 100000
        N_EDGES = 9375
        DIM = 128
        key = jax.random.key(seed)
        k1, k2, k3 = jax.random.split(key, 3)
        x = jax.random.normal(k1, (N_NODES, DIM), dtype=jnp.float32)
        edge_index = jax.random.randint(k2, (2, N_EDGES), 0, N_NODES)
        W = jax.random.normal(k3, (DIM, DIM), dtype=jnp.float32) / np.float32(np.sqrt(DIM))
        b = jnp.zeros((DIM,), dtype=jnp.float32)
        return {'x': x, 'edge_index': edge_index, 'W': W, 'b': b}
    _L1_gnn_all = _L1_gnn_setup()
    _L1_gnn_in = {k: v for k, v in _L1_gnn_all.items() if k in ('W', 'b')}
    del _L1_gnn_all
    return {'x': x, 'src': src, 'dst': dst, 'edge_attr_64': edge_attr_64, 'L0_gnn_mW1': _L0_gnn_in['mW1'], 'L0_gnn_mb1': _L0_gnn_in['mb1'], 'L0_gnn_mW2': _L0_gnn_in['mW2'], 'L0_gnn_mb2': _L0_gnn_in['mb2'], 'L0_gnn_mW3': _L0_gnn_in['mW3'], 'L0_gnn_mb3': _L0_gnn_in['mb3'], 'L0_gnn_uW1': _L0_gnn_in['uW1'], 'L0_gnn_ub1': _L0_gnn_in['ub1'], 'L0_gnn_uW2': _L0_gnn_in['uW2'], 'L0_gnn_ub2': _L0_gnn_in['ub2'], 'L0_gnn_uW3': _L0_gnn_in['uW3'], 'L0_gnn_ub3': _L0_gnn_in['ub3'], 'L1_gnn_W': _L1_gnn_in['W'], 'L1_gnn_b': _L1_gnn_in['b']}

def reference(x, src, dst, edge_attr_64, L0_gnn_mW1, L0_gnn_mb1, L0_gnn_mW2, L0_gnn_mb2, L0_gnn_mW3, L0_gnn_mb3, L0_gnn_uW1, L0_gnn_ub1, L0_gnn_uW2, L0_gnn_ub2, L0_gnn_uW3, L0_gnn_ub3, L1_gnn_W, L1_gnn_b):
    import jax
    import jax.numpy as jnp

    def _L0_gnn_ref(node_states, edges, vertices, mW1, mb1, mW2, mb2, mW3, mb3, uW1, ub1, uW2, ub2, uW3, ub3):
        import jax, jax.numpy as jnp
        import numpy as np
        NUM_NODES = 32
        N = 1024
        E = 8192
        D = 128
        ED = 64
        H = 256
        M = 128
        U = 256

        def _mlp3(x, W1, b1, W2, b2, W3, b3):
            h = jax.nn.relu(x @ W1 + b1)
            h = jax.nn.relu(h @ W2 + b2)
            return h @ W3 + b3
        nodes_i = node_states[vertices[:, 0]]
        nodes_j = node_states[vertices[:, 1]]
        messages = _mlp3(jnp.concatenate([nodes_i, nodes_j, edges], axis=1), mW1, mb1, mW2, mb2, mW3, mb3)
        summed = jax.ops.segment_sum(messages, vertices[:, 0], num_segments=N) + jax.ops.segment_sum(messages, vertices[:, 1], num_segments=N)
        paired = node_states.reshape(-1, 2, NUM_NODES, D)
        attention = jnp.concatenate([paired[:, 0] - paired[:, 1], paired[:, 1] - paired[:, 0]], axis=1).reshape(-1, D)
        upd_in = jnp.concatenate([node_states, summed, attention], axis=1)
        return _mlp3(upd_in, uW1, ub1, uW2, ub2, uW3, ub3)

    def _L1_gnn_ref(x, edge_index, W, b):
        import jax, jax.numpy as jnp
        import numpy as np
        N_NODES = 100000
        N_EDGES = 9375
        DIM = 128
        n = x.shape[0]
        loop = jnp.arange(n, dtype=edge_index.dtype)
        row = jnp.concatenate([edge_index[0], loop])
        col = jnp.concatenate([edge_index[1], loop])
        ones = jnp.ones(row.shape[0], dtype=x.dtype)
        deg = jax.ops.segment_sum(ones, col, num_segments=n)
        dinv = jnp.where(deg > 0, jax.lax.rsqrt(deg), jnp.zeros_like(deg))
        norm = dinv[row] * dinv[col]
        xw = x @ W
        msgs = norm[:, None] * xw[row]
        out = jax.ops.segment_sum(msgs, col, num_segments=n) + b
        return jax.nn.gelu(out, approximate=False)
    edge_index = jnp.stack([src, dst])
    edge_index_t = jnp.stack([src, dst], axis=1)
    h = jnp.maximum(_layernorm(x, axis=-1), 0.0)
    x = x + _L0_gnn_ref(h, edge_attr_64, edge_index_t, L0_gnn_mW1, L0_gnn_mb1, L0_gnn_mW2, L0_gnn_mb2, L0_gnn_mW3, L0_gnn_mb3, L0_gnn_uW1, L0_gnn_ub1, L0_gnn_uW2, L0_gnn_ub2, L0_gnn_uW3, L0_gnn_ub3)
    h = jnp.maximum(_layernorm(x, axis=-1), 0.0)
    x = x + _L1_gnn_ref(h, edge_index, L1_gnn_W, L1_gnn_b)
    return x

_drawn_inputs = setup_inputs


def setup_inputs(seed=0):
    import zlib

    import numpy as np

    out = dict(_drawn_inputs(seed))
    spreads = {'L0_gnn_mb1': (0.0, 0.8),
     'L0_gnn_mb2': (0.0, 0.583),
     'L0_gnn_mb3': (0.0, 0.546),
     'L0_gnn_ub1': (0.0, 2.0),
     'L0_gnn_ub2': (0.0, 1.866),
     'L0_gnn_ub3': (0.0, 0.378),
     'L1_gnn_b': (0.0, 0.585)}
    factors = {'edge_attr_64': 8.0, 'L0_gnn_mW1': 8.0, 'L0_gnn_mW2': 6.681, 'L0_gnn_mW3': 2.912}
    for name, (base, spread) in spreads.items():
        noise = np.random.default_rng([zlib.crc32(name.encode()), seed]).standard_normal(out[name].shape)
        drawn = base * np.exp(spread * noise) if base else spread * noise
        out[name] = jnp.asarray(drawn.astype(out[name].dtype))
    for name, factor in factors.items():
        out[name] = (out[name] * factor).astype(out[name].dtype)
    return out
```

```python
from contextlib import ExitStack

import concourse.bass as bass
from concourse import mybir

P = 128
ALU = mybir.AluOpType
ACT = mybir.ActivationFunctionType
F32 = mybir.dt.float32
F32R = mybir.dt.float32r
BF16 = mybir.dt.bfloat16
F16 = mybir.dt.float16
I32 = mybir.dt.int32
AX_X = mybir.AxisListType.X
LN_EPS = 1e-5


def gnn_preln_kernel(nc, x, src_cols, dst_cols, edge_attr_t, mW1, mb1, mW2, mb2_cols, mW3, mb3,
                     uW1, ub1_cols, uW2, ub2_cols, uW3, ub3, gcn_W, gcn_b, out):
    N, D = x.shape
    TILES = src_cols.shape[1]
    ED = edge_attr_t.shape[0]
    H = mW2.shape[0]
    NC = N // P
    KH = H // P
    GT = 4
    GE = GT * P
    GROUPS = TILES // GT
    HB = 512
    NH = N // HB
    PAIR_ATT = 32
    assert D == P and 2 * ED == P and H == 2 * P and GROUPS % 2 == 0

    table_a = nc.dram_tensor("table_a", [N, H], F32).ap()
    table_b = nc.dram_tensor("table_b", [N, H], F32).ap()

    with ExitStack() as ctx:
        def sb(name, shape, dt=F32):
            return ctx.enter_context(nc.sbuf_tensor(name, shape, dt))

        def sem(name):
            return ctx.enter_context(nc.semaphore(name))

        bank = [ctx.enter_context(nc.psum_tensor(f"bank{i}", [P, HB], F32)) for i in range(8)]
        acc_bank = bank[0:2]
        z1_bank = bank[2:4]
        z1t_bank = bank[4]
        z2_bank = bank[5:7]
        msg_bank = bank[7]

        x_sb = sb("x_sb", [P, NC, D])
        src_i = sb("src_i", [P, TILES], I32)
        dst_i = sb("dst_i", [P, TILES], I32)
        w1_sb = sb("w1_sb", [P, 2, H])
        w1e_sb = sb("w1e_sb", [P, H])
        b1_row = sb("b1_row", [1, H])
        w2_sb = sb("w2_sb", [P, KH, H])
        b2_sb = sb("b2_sb", [P, KH])
        w3_sb = sb("w3_sb", [P, KH, D])
        b3_all = sb("b3_all", [P, D])
        u1_sb = sb("u1_sb", [P, 3, H])
        ub1_sb = sb("ub1_sb", [P, KH])
        u2_sb = sb("u2_sb", [P, KH, H])
        ub2_sb = sb("ub2_sb", [P, KH])
        u3_sb = sb("u3_sb", [P, KH, D])
        ub3_all = sb("ub3_all", [P, D])
        gw_sb = sb("gw_sb", [P, D])
        gb_all = sb("gb_all", [P, D])

        iota_f = sb("iota_f", [P, N])
        iota_h = sb("iota_h", [P, N], F16)
        ident = sb("ident", [P, P])
        ones_bf = sb("ones_bf", [P, P], BF16)
        zeros_bf = sb("zeros_bf", [P, HB], BF16)
        ones_row = sb("ones_row", [1, P])

        w1e_hi = sb("w1e_hi", [P, H], F32R)
        w1e_lo = sb("w1e_lo", [P, H], F32R)
        w2_hi = sb("w2_hi", [P, KH, H], F32R)
        w2_lo = sb("w2_lo", [P, KH, H], F32R)

        stats = sb("stats", [P, NC, 6])
        mv = sb("mv", [P, NC, 2])
        std = sb("std", [P, NC])
        rstd = sb("rstd", [P, NC])
        h_sb = sb("h_sb", [P, NC, D])
        h_t = sb("h_t", [P, N])
        att_t = sb("att_t", [P, N])
        tab_sb = sb("tab_sb", [P, NC, 2, H])
        uh_sb = sb("uh_sb", [P, KH, N])
        xb_sb = sb("xb_sb", [P, NC, D])

        src_f = sb("src_f", [P, TILES])
        dst_f = sb("dst_f", [P, TILES])
        chunk_i = sb("chunk_i", [P, TILES], I32)
        chunk_f = sb("chunk_f", [P, TILES])
        back_iota = sb("back_iota", [1, GROUPS])
        hi_f = sb("hi_f", [1, NC])
        lo_f = sb("lo_f", [1, NC])
        lo2_f = sb("lo2_f", [1, NC])
        len_f = sb("len_f", [1, NC])
        cum_f = sb("cum_f", [1, NC])
        range_i = sb("range_i", [1, NC, 4], I32)

        oh_src_c = sb("oh_src_c", [P, GT, N], BF16)
        oh_dst_c = sb("oh_dst_c", [P, GT, P], BF16)
        c_sb = sb("c_sb", [P, 2, N])
        ct_sb = sb("ct_sb", [P, NC, N])
        deg_in2 = sb("deg_in2", [P, NC, NH])
        deg_in = sb("deg_in", [P, NC])
        deg_out = sb("deg_out", [P, NC])
        cnt = sb("cnt", [P, NC])
        dinv = sb("dinv", [P, NC])
        cb3 = sb("cb3", [P, NC, D])

        gidx = sb("gidx", [P, 2, 2, GT], I32)
        g_sb = sb("g_sb", [P, 2, GT, H])
        e_raw = sb("e_raw", [P, 2, GE])
        e_hl = sb("e_hl", [P, 2, GE], F32R)
        z1_sb = sb("z1_sb", [P, 2, 2, H])
        h1_hi = sb("h1_hi", [P, KH, GE], F32R)
        h1_lo = sb("h1_lo", [P, KH, GE], F32R)
        h2_sb = sb("h2_sb", [P, KH, GE])
        m_hi = sb("m_hi", [P, 2, GT, D], F32R)
        m_lo = sb("m_lo", [P, 2, GT, D], F32R)
        oh_s = oh_src_c[:, 0, :]
        oh_d = oh_src_c[:, 1, :]
        oh_sum = oh_src_c[:, 2:4, :]
        inc = sb("inc", [P, 2, GT, N], F32R)

        spare = z1_sb[:, :, :, :].rearrange("p q t n -> p (q t n)")
        grp = z1_sb[0:1, 0, :, :].rearrange("p t n -> p (t n)").rearrange("p (c g) -> p c g", c=NC)
        grp_w = z1_sb[0:1, 1, :, :].rearrange("p t n -> p (t n)").rearrange("p (c g) -> p c g", c=NC)
        in_chunk = g_sb[:, 0, :, :].rearrange("p t n -> p (t n)").bitcast(BF16).rearrange("p (c t) -> p c t", c=NC)
        tab_all = tab_sb[:, :, :, :].rearrange("p c t n -> p (c t n)")
        u_a = tab_all[:, 0:KH * N].rearrange("p (k n) -> p k n", k=KH)
        sum_t = tab_all[:, KH * N:KH * N + N]
        x1_sb = tab_all[:, KH * N + N:KH * N + 2 * N].rearrange("p (c d) -> p c d", c=NC)
        y_sb = c_sb[:, 0, :].rearrange("p (c d) -> p c d", c=NC)
        o_sb = c_sb[:, 1, :].rearrange("p (c d) -> p c d", c=NC)

        ld_x = sem("ld_x")
        ld_idx = sem("ld_idx")
        ld_w = sem("ld_w")
        consts_pool = sem("consts_pool")
        pool_step = sem("pool_step")
        dve_step = sem("dve_step")
        var_ready = sem("var_ready")
        std_ready = sem("std_ready")
        h_ready = sem("h_ready")
        ht_psum = sem("ht_psum")
        ht_ready = sem("ht_ready")
        att_ready = sem("att_ready")
        tab_psum = sem("tab_psum")
        tab_ready = sem("tab_ready")
        tab_stored = sem("tab_stored")
        uh_psum = sem("uh_psum")
        uh_ready = sem("uh_ready")
        chunks_marked = sem("chunks_marked")
        marks_psum = sem("marks_psum")
        ranges_ready = sem("ranges_ready")
        ends_ready = sem("ends_ready")
        split_ready = sem("split_ready")
        c_hot = sem("c_hot")
        c_used = sem("c_used")
        c_psum = sem("c_psum")
        c_ready = sem("c_ready")
        ct_psum = sem("ct_psum")
        ct_ready = sem("ct_ready")
        degs_ready = sem("degs_ready")
        sqrt_ready = sem("sqrt_ready")
        cb3_ready = sem("cb3_ready")
        gidx_ready = sem("gidx_ready")
        ga_done = [[sem(f"ga_done{b}_{j}") for j in range(GT)] for b in range(2)]
        gb_done = [[sem(f"gb_done{b}_{j}") for j in range(GT)] for b in range(2)]
        e_loaded = [sem("e_loaded0"), sem("e_loaded1")]
        e_cast = sem("e_cast")
        e_ready = sem("e_ready")
        z1_psum = sem("z1_psum")
        z1_ready = sem("z1_ready")
        z1t_psum = sem("z1t_psum")
        h1_hi_ready = sem("h1_hi_ready")
        h1_lo_ready = sem("h1_lo_ready")
        z2_psum = sem("z2_psum")
        h2_ready = sem("h2_ready")
        m_psum = sem("m_psum")
        m_hi_ready = sem("m_hi_ready")
        m_lo_ready = sem("m_lo_ready")
        oh_made = sem("oh_made")
        oh_added = sem("oh_added")
        inc_ready = sem("inc_ready")
        scattered = sem("scattered")
        sum_ready = sem("sum_ready")
        u1_psum = sem("u1_psum")
        u1_added = sem("u1_added")
        u1_ready = sem("u1_ready")
        u2_psum = sem("u2_psum")
        u2_ready = sem("u2_ready")
        u3_psum = sem("u3_psum")
        x1_ready = sem("x1_ready")
        var2_ready = sem("var2_ready")
        std2_ready = sem("std2_ready")
        h2n_ready = sem("h2n_ready")
        h2t_psum = sem("h2t_psum")
        h2t_ready = sem("h2t_ready")
        xw_psum = sem("xw_psum")
        y_ready = sem("y_ready")
        agg_psum = sem("agg_psum")
        pre_ready = sem("pre_ready")
        gelu_ready = sem("gelu_ready")
        out_ready = sem("out_ready")
        stored = sem("stored")

        block = ctx.enter_context(nc.Block())

        @block.sync
        def _(sp):
            sp.dma_start(x_sb[:, :, :], x.rearrange("(c p) d -> p c d", p=P)).then_inc(ld_x, 16)
            sp.dma_start(dst_i[:, :], dst_cols).then_inc(ld_idx, 16)
            sp.dma_start(src_i[:, :], src_cols).then_inc(ld_idx, 16)
            loads = [
                (w1_sb[:, :, :], mW1[0:2 * D, :].rearrange("(k p) n -> p k n", p=P)),
                (b1_row[:, :], mb1),
                (w1e_sb[0:ED, :], mW1[2 * D:2 * D + ED, :]),
                (w1e_sb[ED:P, :], mW1[2 * D:2 * D + ED, :]),
                (u1_sb[:, :, :], uW1.rearrange("(k p) n -> p k n", p=P)),
                (ub1_sb[:, :], ub1_cols),
                (w2_sb[:, :, :], mW2.rearrange("(k p) n -> p k n", p=P)),
                (b2_sb[:, :], mb2_cols),
                (w3_sb[:, :, :], mW3.rearrange("(k p) n -> p k n", p=P)),
                (b3_all[:, :], mb3.partition_broadcast(P)),
                (u2_sb[:, :, :], uW2.rearrange("(k p) n -> p k n", p=P)),
                (ub2_sb[:, :], ub2_cols),
                (u3_sb[:, :, :], uW3.rearrange("(k p) n -> p k n", p=P)),
                (ub3_all[:, :], ub3.partition_broadcast(P)),
                (gw_sb[:, :], gcn_W),
                (gb_all[:, :], gcn_b.partition_broadcast(P)),
            ]
            for to, frm in loads:
                sp.dma_start(to, frm).then_inc(ld_w, 16)

            def load_edges(g, b):
                cols = edge_attr_t[:, bass.ds(g * GE, GE)]
                sp.dma_start(e_raw[0:ED, b, :], cols).then_inc(e_loaded[b], 16)
                sp.dma_start(e_raw[ED:P, b, :], cols).then_inc(e_loaded[b], 16)

            load_edges(0, 0)
            load_edges(1, 1)
            sp.wait_ge(tab_ready, NC)
            sp.dma_start(table_a.rearrange("(c p) n -> p c n", p=P), tab_sb[:, :, 0, :]).then_inc(tab_stored, 16)
            sp.dma_start(table_b.rearrange("(c p) n -> p c n", p=P), tab_sb[:, :, 1, :]).then_inc(tab_stored, 16)
            with sp.Fori(0, GROUPS // 2 - 1) as i:
                for b in range(2):
                    sp.wait_ge(e_ready, 2 * i + b + 1)
                    load_edges(2 * i + b + 2, b)
            for half in range(NH):
                sp.wait_ge(out_ready, half + 1)
                c0, c1 = half * NC // NH, (half + 1) * NC // NH
                sp.dma_start(out[c0 * P:c1 * P, :].rearrange("(c p) d -> p c d", p=P),
                             o_sb[:, c0:c1, :]).then_inc(stored, 16)
            sp.wait_ge(stored, 16 * NH)

        @block.gpsimd
        def _(pool):
            steps = [0]

            def step(ins):
                steps[0] += 1
                ins.then_inc(pool_step, 1)
                pool.wait_ge(pool_step, steps[0])

            nc.gpsimd.iota(iota_f[:, :], pattern=[[1, N]], base=0, channel_multiplier=0,
                           allow_small_or_imprecise_dtypes=True).then_inc(consts_pool, 1)
            nc.gpsimd.memset(ones_bf[:, :], 1.0).then_inc(consts_pool, 1)
            nc.gpsimd.memset(zeros_bf[:, :], 0.0).then_inc(consts_pool, 1)
            nc.gpsimd.memset(ones_row[:, :], 1.0).then_inc(consts_pool, 1)
            nc.gpsimd.iota(back_iota[:, :], pattern=[[-1, GROUPS]], base=GROUPS, channel_multiplier=0,
                           allow_small_or_imprecise_dtypes=True).then_inc(consts_pool, 1)
            step(nc.gpsimd.memset(ident[:, :], 0.0))
            nc.gpsimd.affine_select(out=ident[:, :], in_=ident[:, :], compare_op=ALU.not_equal, fill=1.0,
                                    base=0, pattern=[[-1, P]], channel_multiplier=1).then_inc(consts_pool, 1)
            pool.wait_ge(ld_idx, 32)

            def gather_group(g, b, n):
                copied = 2 * g + 2
                landed = 16 * (n + 1)
                if not isinstance(g, int):
                    copied, landed = pool.to_reg(copied), pool.to_reg(landed)
                nc.gpsimd.tensor_copy(gidx[:, b, 0, :], src_i[:, bass.ds(g * GT, GT)]).then_inc(gidx_ready, 1)
                nc.gpsimd.tensor_copy(gidx[:, b, 1, :], dst_i[:, bass.ds(g * GT, GT)]).then_inc(gidx_ready, 1)
                pool.wait_ge(tab_stored, 32)
                pool.wait_ge(gidx_ready, copied)
                for j in range(GT):
                    nc.gpsimd.indirect_dma_start(
                        g_sb[:, b, j, :], None, table_a,
                        bass.IndirectOffsetOnAxis(ap=gidx[:, b, 0, j:j + 1], axis=0),
                    ).then_inc(ga_done[b][j], 16)
                for j in range(GT):
                    pool.wait_ge(tab_stored, 32)
                    pool.wait_ge(ga_done[b][j], landed)
                    nc.gpsimd.indirect_dma_start(
                        g_sb[:, b, j, :], None, table_b,
                        bass.IndirectOffsetOnAxis(ap=gidx[:, b, 1, j:j + 1], axis=0), compute_op=ALU.add,
                    ).then_inc(gb_done[b][j], 16)

            for b in range(2):
                gather_group(b, b, 0)
            with pool.Fori(1, GROUPS // 2) as i:
                for b in range(2):
                    g = 2 * i + b
                    for j in range(GT):
                        pool.wait_ge(gb_done[b][j], 16 * i)
                    pool.wait_ge(z1_ready, 2 * (g - 1))
                    gather_group(g, b, i)

        @block.tensor
        def _(pe):
            pe.wait_ge(consts_pool, 6)
            pe.wait_ge(chunks_marked, 1)
            marks = in_chunk.rearrange("p c t -> p (c t)")
            for q in range(4):
                mm = nc.tensor.matmul(bank[4 + q][0:1, :], ones_bf[:, 0:1], marks[:, q * HB:(q + 1) * HB],
                                      start=True, stop=True)
            mm.then_inc(marks_psum, 1)
            pe.wait_ge(h_ready, 1)
            for c in range(NC):
                mm = nc.tensor.transpose(bank[c // 4][:, (c % 4) * P:(c % 4 + 1) * P], h_sb[:, c, :], ident[:, :])
            mm.then_inc(ht_psum, 1)
            pe.wait_ge(ht_ready, 1)
            pe.wait_ge(ld_w, 16 * 16)
            for c in range(NC):
                if c >= 2:
                    pe.wait_ge(tab_ready, c - 1)
                to = bank[2 + c % 2]
                hc = h_t[:, c * P:(c + 1) * P]
                nc.tensor.matmul(to[:, 0:H], hc, w1_sb[:, 0, :], start=True, stop=False, skip_group_check=True)
                nc.tensor.matmul(to[:, 0:H], ones_row[:, :], b1_row[:, :], start=False, stop=True,
                                 skip_group_check=True)
                nc.tensor.matmul(to[:, H:2 * H], hc, w1_sb[:, 1, :], start=False, stop=True,
                                 skip_group_check=True).then_inc(tab_psum, 1)
            pe.wait_ge(att_ready, 1)
            for k in range(KH * NH):
                m, n = k // NH, k % NH
                if k >= 2:
                    pe.wait_ge(uh_ready, k - 1)
                to = bank[k % 2]
                nc.tensor.matmul(to[:, :], u1_sb[:, 0, m * P:(m + 1) * P], h_t[:, n * HB:(n + 1) * HB],
                                 start=True, stop=False)
                nc.tensor.matmul(to[:, :], u1_sb[:, 2, m * P:(m + 1) * P], att_t[:, n * HB:(n + 1) * HB],
                                 start=False, stop=True).then_inc(uh_psum, 1)
            pe.wait_ge(uh_ready, KH * NH)
            pe.wait_ge(tab_ready, NC)
            pe.wait_ge(ranges_ready, 1)
            for c in range(NC):
                first_visit = pe.value_load(range_i[0:1, c, 0:1], min_val=0, max_val=NC * GROUPS)
                end_visit = pe.value_load(range_i[0:1, c, 1:2], min_val=1, max_val=NC * GROUPS)
                cb = bank[2 * (c % 2):2 * (c % 2) + 2]
                if c >= 2:
                    pe.wait_ge(c_ready, c - 1)
                for n in range(NH):
                    nc.tensor.matmul(cb[n][:, :], zeros_bf[:, 0:P], zeros_bf[:, :], start=True, stop=False,
                                     skip_group_check=True)
                with pe.Fori(first_visit, end_visit) as visit:
                    for j in range(GT):
                        pe.wait_ge(c_hot, visit * GT + (j + 1))
                        for n in range(NH):
                            mm = nc.tensor.matmul(cb[n][:, :], oh_dst_c[:, j, :],
                                                  oh_src_c[:, j, n * HB:(n + 1) * HB],
                                                  start=False, stop=False, skip_group_check=True)
                        mm.then_inc(c_used, 1)
                for n in range(NH):
                    mm = nc.tensor.matmul(cb[n][:, :], zeros_bf[:, 0:P], zeros_bf[:, :], start=False, stop=True,
                                          skip_group_check=True)
                mm.then_inc(c_psum, 1)
                for cc in ([c - 1] if c else []) + ([c] if c == NC - 1 else []):
                    pe.wait_ge(c_ready, cc + 1)
                    if cc:
                        pe.wait_ge(ct_ready, cc)
                    for s in range(NC):
                        mm = nc.tensor.transpose(bank[4 + s // 4][:, (s % 4) * P:(s % 4 + 1) * P],
                                                 c_sb[:, cc % 2, s * P:(s + 1) * P], ident[:, :])
                    mm.then_inc(ct_psum, 1)

            pe.wait_ge(cb3_ready, 1)
            pe.wait_ge(ct_ready, NC)
            for c in range(NC):
                nc.tensor.matmul(acc_bank[c // 4][:, (c % 4) * P:(c % 4 + 1) * P], cb3[:, c, :], ident[:, :],
                                 start=(c % 4 == 0), stop=False, skip_group_check=True)
            pe.wait_ge(split_ready, 1)

            def first_layer(g, b):
                pe.wait_ge(e_ready, g + 1)
                for q in range(2):
                    for t in range(2):
                        ee = e_hl[:, b, (2 * q + t) * P:(2 * q + t + 1) * P]
                        to = z1_bank[q][:, t * H:(t + 1) * H]
                        nc.tensor.matmul(to, ee, w1e_hi[:, :], start=(t == 0), stop=False, skip_group_check=True)
                        mm = nc.tensor.matmul(to, ee, w1e_lo[:, :], start=False, stop=True, skip_group_check=True)
                    mm.then_inc(z1_psum, 1)

            def transpose_pair(g, q, first=False):
                pe.wait_ge(z1_ready, 2 * g + q + 1)
                if not (first and q == 0):
                    pe.wait_ge(h1_lo_ready, 2 * g + q)
                for k in range(KH):
                    for t in range(2):
                        mm = nc.tensor.transpose(z1t_bank[:, (2 * k + t) * P:(2 * k + t + 1) * P],
                                                 z1_sb[:, q, t, k * P:(k + 1) * P], ident[:, :])
                mm.then_inc(z1t_psum, 1)

            def second_layer(g, first=False):
                pe.wait_ge(h1_lo_ready, 2 * g + 2)
                for m in range(KH):
                    if not first:
                        pe.wait_ge(h2_ready, 2 * g + m - 1)
                    parts = [(w, a, k) for w, a in ((w2_hi, h1_hi), (w2_lo, h1_hi), (w2_hi, h1_lo)) for k in range(KH)]
                    for n, (w, a, k) in enumerate(parts):
                        mm = nc.tensor.matmul(z2_bank[m][:, :], w[:, k, m * P:(m + 1) * P], a[:, k, :],
                                              start=(n == 0), stop=(n == len(parts) - 1))
                    mm.then_inc(z2_psum, 1)

            def messages(g, tiles, first=False):
                if tiles[0] == 0:
                    pe.wait_ge(h2_ready, 2 * g + 2)
                    if not first:
                        pe.wait_ge(m_lo_ready, g)
                for t in tiles:
                    for k in range(KH):
                        mm = nc.tensor.matmul(msg_bank[:, t * D:(t + 1) * D], h2_sb[:, k, t * P:(t + 1) * P],
                                              w3_sb[:, k, :], start=(t == 0 and k == 0), stop=(k == KH - 1),
                                              skip_group_check=True)
                mm.then_inc(m_psum, 1)

            def scatter(g, b, tiles):
                pe.wait_ge(m_lo_ready, g + 1)
                for t in tiles:
                    pe.wait_ge(inc_ready, GT * g + (t + 1))
                    for part in (m_hi, m_lo):
                        for n in range(NH):
                            mm = nc.tensor.matmul(acc_bank[n][:, :], part[:, b, t, :],
                                                  inc[:, b, t, n * HB:(n + 1) * HB],
                                                  start=False, stop=False, skip_group_check=True)
                    mm.then_inc(scattered, 1)

            def group(g, b, first=False, last=False):
                second_layer(g, first)
                if not last:
                    first_layer(g + 1, 1 - b)
                messages(g, (0, 1), first)
                if not last:
                    transpose_pair(g + 1, 0)
                messages(g, (2, 3), first)
                if not first:
                    scatter(g - 1, 1 - b, (0,))
                if not last:
                    transpose_pair(g + 1, 1)
                if not first:
                    scatter(g - 1, 1 - b, (1, 2, 3))

            first_layer(0, 0)
            transpose_pair(0, 0, first=True)
            transpose_pair(0, 1, first=True)
            group(0, 0, first=True)
            with pe.Fori(0, (GROUPS - 2) // 2) as i:
                group(2 * i + 1, 1)
                group(2 * i + 2, 0)
            group(GROUPS - 1, 1, last=True)
            scatter(GROUPS - 1, 1, range(GT))

            for k in range(KH * NH):
                m, n = k // NH, k % NH
                if m == 0:
                    pe.wait_ge(sum_ready, n + 1)
                nc.tensor.matmul(bank[2 + k][:, :], u1_sb[:, 1, m * P:(m + 1) * P], sum_t[:, n * HB:(n + 1) * HB],
                                 start=True, stop=True).then_inc(u1_psum, 1)
            u2_bank = [bank[0], bank[1], bank[6], bank[7]]
            pe.wait_ge(u1_ready, KH * NH)
            for k in range(KH * NH):
                m, n = k // NH, k % NH
                for kk in range(KH):
                    mm = nc.tensor.matmul(u2_bank[k][:, :], u2_sb[:, kk, m * P:(m + 1) * P],
                                          uh_sb[:, kk, n * HB:(n + 1) * HB], start=(kk == 0), stop=(kk == KH - 1))
                mm.then_inc(u2_psum, 1)
            pe.wait_ge(u2_ready, KH * NH)
            for c in range(NC):
                for kk in range(KH):
                    mm = nc.tensor.matmul(bank[2 + c // 4][:, (c % 4) * D:(c % 4 + 1) * D],
                                          u_a[:, kk, c * P:(c + 1) * P], u3_sb[:, kk, :],
                                          start=(kk == 0 and c % 4 == 0), stop=(kk == KH - 1), skip_group_check=True)
                mm.then_inc(u3_psum, 1)
            pe.wait_ge(h2n_ready, 1)
            for c in range(NC):
                mm = nc.tensor.transpose(bank[4 + c // 4][:, (c % 4) * P:(c % 4 + 1) * P], h_sb[:, c, :], ident[:, :])
            mm.then_inc(h2t_psum, 1)
            pe.wait_ge(h2t_ready, 1)
            for c in range(NC):
                mm = nc.tensor.matmul(bank[6 + c // 4][:, (c % 4) * D:(c % 4 + 1) * D], h_t[:, c * P:(c + 1) * P],
                                      gw_sb[:, :], start=(c % 4 == 0), stop=True, skip_group_check=True)
                mm.then_inc(xw_psum, 1)
            pe.wait_ge(y_ready, NC)
            for c in range(NC):
                for s in range(NC):
                    mm = nc.tensor.matmul(bank[c // 4][:, (c % 4) * D:(c % 4 + 1) * D],
                                          ct_sb[:, s, c * P:(c + 1) * P], y_sb[:, s, :],
                                          start=(s == 0 and c % 4 == 0), stop=(s == NC - 1), skip_group_check=True)
                mm.then_inc(agg_psum, 1)

        @block.scalar
        def _(act):
            act.wait_ge(var_ready, 1)
            nc.scalar.activation(std[:, :], std[:, :], ACT.Sqrt).then_inc(std_ready, 1)
            act.wait_ge(ht_psum, 1)
            nc.scalar.copy(h_t[:, 0:HB], bank[0][:, :])
            nc.scalar.copy(h_t[:, HB:N], bank[1][:, :]).then_inc(ht_ready, 1)
            for c in range(NC):
                act.wait_ge(tab_psum, c + 1)
                nc.scalar.copy(tab_sb[:, c, :, :].rearrange("p t n -> p (t n)"), bank[2 + c % 2][:, :]).then_inc(tab_ready, 1)
            for k in range(KH * NH):
                m, n = k // NH, k % NH
                act.wait_ge(uh_psum, k + 1)
                nc.scalar.activation(uh_sb[:, m, n * HB:(n + 1) * HB], bank[k % 2][:, :], ACT.Identity,
                                     bias=ub1_sb[:, m:m + 1]).then_inc(uh_ready, 1)

            def split_edges(g, b, n):
                act.wait_ge(e_loaded[b], 32 * (n + 1))
                nc.scalar.copy(e_hl[:, b, :], e_raw[:, b, :]).then_inc(e_cast, 1)

            for c in range(NC):
                act.wait_ge(c_psum, c + 1)
                if c >= 2:
                    act.wait_ge(ct_psum, c - 1)
                for n in range(NH):
                    cp = nc.scalar.activation(c_sb[:, c % 2, n * HB:(n + 1) * HB], bank[2 * (c % 2) + n][:, :],
                                              ACT.Copy, accum_out=deg_in2[:, c, n:n + 1])
                cp.then_inc(c_ready, 1)
                if c:
                    for n in range(NH):
                        if n == 0:
                            act.wait_ge(ct_psum, c)
                        cp = nc.scalar.copy(ct_sb[:, 4 * n:4 * n + 4, (c - 1) * P:c * P],
                                            bank[4 + n][:, :].rearrange("p (s d) -> p s d", s=4))
                    cp.then_inc(ct_ready, 1)
            act.wait_ge(ct_psum, NC)
            for n in range(NH):
                cp = nc.scalar.copy(ct_sb[:, 4 * n:4 * n + 4, (NC - 1) * P:NC * P],
                                    bank[4 + n][:, :].rearrange("p (s d) -> p s d", s=4))
            cp.then_inc(ct_ready, 1)
            act.wait_ge(ct_ready, NC)
            for s in range(NC):
                if s:
                    act.wait_ge(degs_ready, s)
                nc.scalar.activation(spare, ct_sb[:, s, :], ACT.Copy, accum_out=deg_out[:, s:s + 1]).then_inc(degs_ready, 1)
            act.wait_ge(cb3_ready, 1)
            nc.scalar.activation(dinv[:, :], dinv[:, :], ACT.Sqrt).then_inc(sqrt_ready, 1)
            split_edges(0, 0, 0)
            split_edges(1, 1, 0)

            def relu_pair(g, q, first=False):
                act.wait_ge(z1t_psum, 2 * g + q + 1)
                if not first:
                    act.wait_ge(z2_psum, 2 * g)
                nc.scalar.activation(h1_hi[:, :, q * 2 * P:(q + 1) * 2 * P],
                                     z1t_bank[:, :].rearrange("p (k e) -> p k e", k=KH), ACT.Relu).then_inc(h1_hi_ready, 1)

            def relu_second(g, m, first=False):
                act.wait_ge(z2_psum, 2 * g + m + 1)
                if not first:
                    act.wait_ge(m_psum, 2 * g)
                nc.scalar.activation(h2_sb[:, m, :], z2_bank[m][:, :], ACT.Relu, bias=b2_sb[:, m:m + 1]).then_inc(h2_ready, 1)

            def cast_inc(g, b, t, first=False):
                act.wait_ge(oh_added, GT * g + t + 1)
                if not first:
                    act.wait_ge(scattered, GT * (g - 2) + t + 1)
                nc.scalar.copy(inc[:, b, t, :], oh_sum[:, t % 2, :]).then_inc(inc_ready, 1)

            def high_messages(g, b, first=False):
                act.wait_ge(m_psum, 2 * g + 2)
                if not first:
                    act.wait_ge(scattered, GT * (g - 1))
                nc.scalar.copy(m_hi[:, b, :, :].rearrange("p t d -> p (t d)"), msg_bank[:, :]).then_inc(m_hi_ready, 1)

            def group(g, b, n, first=False, second=False, last=False, last_two=False):
                relu_second(g, 0, first)
                cast_inc(g, b, 0, first or second)
                relu_second(g, 1, first)
                cast_inc(g, b, 1, first or second)
                if not last:
                    relu_pair(g + 1, 0)
                high_messages(g, b, first or second)
                if not last:
                    relu_pair(g + 1, 1)
                if not last_two:
                    act.wait_ge(z1_psum, 2 * g + 2)
                    split_edges(g + 2, b, n + 1)
                cast_inc(g, b, 2, first or second)
                cast_inc(g, b, 3, first or second)

            relu_pair(0, 0, first=True)
            relu_pair(0, 1, first=True)
            group(0, 0, 0, first=True)
            group(1, 1, 0, second=True)
            with act.Fori(1, GROUPS // 2 - 1) as i:
                group(2 * i, 0, i)
                group(2 * i + 1, 1, i)
            group(GROUPS - 2, 0, 0, last_two=True)
            group(GROUPS - 1, 1, 0, last=True, last_two=True)

            for n in range(NH):
                act.wait_ge(scattered, GT * GROUPS)
                nc.scalar.copy(sum_t[:, n * HB:(n + 1) * HB], acc_bank[n][:, :]).then_inc(sum_ready, 1)
            for k in range(KH * NH):
                m, n = k // NH, k % NH
                act.wait_ge(u1_added, k + 1)
                nc.scalar.activation(uh_sb[:, m, n * HB:(n + 1) * HB], uh_sb[:, m, n * HB:(n + 1) * HB],
                                     ACT.Relu).then_inc(u1_ready, 1)
            u2_bank = [bank[0], bank[1], bank[6], bank[7]]
            for k in range(KH * NH):
                m, n = k // NH, k % NH
                act.wait_ge(u2_psum, k + 1)
                nc.scalar.activation(u_a[:, m, n * HB:(n + 1) * HB], u2_bank[k][:, :], ACT.Relu,
                                     bias=ub2_sb[:, m:m + 1]).then_inc(u2_ready, 1)
            act.wait_ge(var2_ready, 1)
            nc.scalar.activation(std[:, :], std[:, :], ACT.Sqrt).then_inc(std2_ready, 1)
            act.wait_ge(h2t_psum, 1)
            nc.scalar.copy(h_t[:, 0:HB], bank[4][:, :])
            nc.scalar.copy(h_t[:, HB:N], bank[5][:, :]).then_inc(h2t_ready, 1)
            for half in range(NH):
                c0, c1 = half * NC // NH, (half + 1) * NC // NH
                act.wait_ge(pre_ready, c1)
                nc.scalar.activation(o_sb[:, c0:c1, :], o_sb[:, c0:c1, :], ACT.Gelu).then_inc(gelu_ready, 1)

        @block.vector
        def _(dve):
            steps = [0]

            def step(ins):
                steps[0] += 1
                ins.then_inc(dve_step, 1)

            def settle():
                dve.wait_ge(dve_step, steps[0])

            def layer_norm(rows, ready, done, final):
                for c in range(NC):
                    step(nc.vector.bn_stats(stats[:, c, :], rows[:, c, :]))
                settle()
                for c in range(NC):
                    step(nc.vector.bn_aggr(mv[:, c, :], stats[:, c, :]))
                settle()
                nc.vector.tensor_scalar(std[:, :], mv[:, :, 1], LN_EPS, None, ALU.add).then_inc(ready, 1)
                for c in range(NC):
                    step(nc.vector.tensor_scalar(h_sb[:, c, :], rows[:, c, :], mv[:, c, 0:1], 0.0,
                                                 ALU.subtract, ALU.max))
                dve.wait_ge(done, 1)
                step(nc.vector.reciprocal(rstd[:, :], std[:, :]))
                settle()
                for c in range(NC):
                    hh = nc.vector.tensor_scalar(h_sb[:, c, :], h_sb[:, c, :], rstd[:, c:c + 1], None, ALU.mult)
                hh.then_inc(final, 1)

            dve.wait_ge(ld_idx, 32)
            step(nc.vector.tensor_scalar(chunk_i[:, :], dst_i[:, :], 7, None, ALU.arith_shift_right))
            nc.vector.tensor_copy(src_f[:, :], src_i[:, :]).then_inc(ends_ready, 1)
            nc.vector.tensor_copy(dst_f[:, :], dst_i[:, :]).then_inc(ends_ready, 1)
            settle()
            step(nc.vector.tensor_copy(chunk_f[:, :], chunk_i[:, :]))
            settle()
            for c in range(NC):
                mark = nc.vector.tensor_scalar(in_chunk[:, c, :], chunk_f[:, :], float(c), None, ALU.is_equal)
            mark.then_inc(chunks_marked, 1)
            dve.wait_ge(ld_x, 16)
            layer_norm(x_sb, var_ready, std_ready, h_ready)
            dve.wait_ge(marks_psum, 1)
            dve.wait_ge(consts_pool, 6)
            per_bank = HB // TILES
            for q in range(4):
                step(nc.vector.tensor_reduce(grp[:, per_bank * q:per_bank * (q + 1), :],
                                             bank[4 + q][0:1, :].rearrange("p (c g t) -> p c g t", c=per_bank, t=GT),
                                             AX_X, ALU.max))
            settle()
            step(nc.vector.tensor_scalar(grp[:, :, :], grp[:, :, :], 1.0, None, ALU.min))
            settle()
            step(nc.vector.tensor_tensor(grp_w[:, :, :], grp[:, :, :],
                                         back_iota[:, :].unsqueeze(1).broadcast_to([1, NC, GROUPS]), ALU.mult))
            settle()
            step(nc.vector.tensor_reduce(lo_f[:, :], grp_w[:, :, :], AX_X, ALU.max))
            settle()
            step(nc.vector.tensor_tensor(grp_w[:, :, :], grp[:, :, :],
                                         iota_f[0:1, 1:GROUPS + 1].unsqueeze(1).broadcast_to([1, NC, GROUPS]), ALU.mult))
            settle()
            step(nc.vector.tensor_reduce(hi_f[:, :], grp_w[:, :, :], AX_X, ALU.max))
            settle()
            step(nc.vector.tensor_scalar(hi_f[:, :], hi_f[:, :], 1.0, None, ALU.max))
            step(nc.vector.tensor_scalar(lo_f[:, :], lo_f[:, :], -1.0, float(GROUPS), ALU.mult, ALU.add))
            settle()
            step(nc.vector.tensor_scalar(len_f[:, :], hi_f[:, :], -1.0, None, ALU.add))
            settle()
            step(nc.vector.tensor_tensor(lo2_f[:, :], lo_f[:, :], len_f[:, :], ALU.min))
            settle()
            step(nc.vector.tensor_tensor(len_f[:, :], hi_f[:, :], lo2_f[:, :], ALU.subtract))
            step(nc.vector.memset(cum_f[:, 0:1], 0.0))
            settle()
            for c in range(1, NC):
                step(nc.vector.tensor_tensor(cum_f[:, c:c + 1], cum_f[:, c - 1:c], len_f[:, c - 1:c], ALU.add))
                settle()
            step(nc.vector.tensor_tensor(hi_f[:, :], cum_f[:, :], len_f[:, :], ALU.add))
            step(nc.vector.tensor_tensor(lo_f[:, :], lo2_f[:, :], cum_f[:, :], ALU.subtract))
            settle()
            step(nc.vector.tensor_copy(range_i[:, :, 0], cum_f[:, :]))
            step(nc.vector.tensor_copy(range_i[:, :, 1], hi_f[:, :]))
            step(nc.vector.tensor_copy(range_i[:, :, 2], lo_f[:, :]))
            settle()
            step(nc.vector.tensor_copy(iota_h[:, :], iota_f[:, :]))
            dve.wait_ge(ht_ready, 1)
            h_pair = h_t[:, :].rearrange("p (b a n) -> p b a n", a=2, n=PAIR_ATT)
            a_pair = att_t[:, :].rearrange("p (b a n) -> p b a n", a=2, n=PAIR_ATT)
            for a in range(2):
                at = nc.vector.tensor_tensor(a_pair[:, :, a, :], h_pair[:, :, a, :], h_pair[:, :, 1 - a, :], ALU.subtract)
            at.then_inc(att_ready, 1)
            dve.wait_ge(ld_w, 16 * 16)
            step(nc.vector.tensor_copy(w1e_hi[:, :], w1e_sb[:, :]))
            step(nc.vector.tensor_copy(w2_hi[:, :, :], w2_sb[:, :, :]))
            settle()
            nc.vector.tensor_tensor(w1e_lo[:, :], w1e_sb[:, :], w1e_hi[:, :].bitcast(F32), ALU.subtract)
            nc.vector.tensor_tensor(w2_lo[:, :, :], w2_sb[:, :, :], w2_hi[:, :, :].bitcast(F32),
                                    ALU.subtract).then_inc(split_ready, 1)
            step(nc.vector.tensor_tensor(xb_sb[:, :, :], x_sb[:, :, :],
                                         ub3_all[:, :].unsqueeze(1).broadcast_to([P, NC, D]), ALU.add))
            dve.wait_ge(ends_ready, 2)
            settle()
            nc.vector.tensor_copy(range_i[:, :, 3], hi_f[:, :]).then_inc(ranges_ready, 1)
            dve.wait_ge(ranges_ready, 1)
            for c in range(NC):
                first_visit = dve.value_load(range_i[0:1, c, 0:1], min_val=0, max_val=NC * GROUPS)
                end_visit = dve.value_load(range_i[0:1, c, 1:2], min_val=1, max_val=NC * GROUPS)
                shift = dve.value_load(range_i[0:1, c, 2:3], min_val=-NC * GROUPS, max_val=GROUPS)
                if c == 0:
                    for j in range(GT):
                        nc.vector.memset(oh_dst_c[:, j, :], 0.0).then_inc(c_used, 1)
                with dve.Fori(first_visit, end_visit) as visit:
                    group_no = nc.s_assert_within(
                        visit + shift, 0, GROUPS - 1,
                        skip_runtime_bounds_check_because="visits of a chunk run over its range of groups")
                    tile0 = group_no * GT
                    for j in range(GT):
                        dve.wait_ge(c_used, visit * GT + (j + 1))
                        nc.vector.tensor_scalar(oh_dst_c[:, j, :], iota_h[:, c * P:(c + 1) * P],
                                                dst_f[:, bass.ds(tile0 + j, 1)], None, ALU.is_equal)
                        nc.vector.tensor_scalar(oh_src_c[:, j, :], iota_h[:, :],
                                                src_f[:, bass.ds(tile0 + j, 1)], None,
                                                ALU.is_equal).then_inc(c_hot, 1)
            dve.wait_ge(degs_ready, NC)
            step(nc.vector.tensor_tensor(deg_in[:, :], deg_in2[:, :, 0], deg_in2[:, :, 1], ALU.add))
            settle()
            step(nc.vector.tensor_tensor(cnt[:, :], deg_in[:, :], deg_out[:, :], ALU.add))
            step(nc.vector.tensor_scalar(deg_in[:, :], deg_in[:, :], 1.0, None, ALU.add))
            settle()
            nc.vector.reciprocal(dinv[:, :], deg_in[:, :])
            for c in range(NC):
                cb = nc.vector.tensor_scalar(cb3[:, c, :], b3_all[:, :], cnt[:, c:c + 1], None, ALU.mult)
            cb.then_inc(cb3_ready, 1)

            def low_edges(g, b):
                dve.wait_ge(e_cast, g + 1)
                nc.vector.tensor_tensor(e_hl[ED:P, b, :], e_raw[ED:P, b, :], e_hl[ED:P, b, :].bitcast(F32),
                                        ALU.subtract).then_inc(e_ready, 1)

            def add_gathered(g, b, q, n, first=False):
                dve.wait_ge(z1_psum, 2 * g + q + 1)
                for t in range(2):
                    dve.wait_ge(gb_done[b][2 * q + t], 16 * (n + 1))
                if not first:
                    dve.wait_ge(z1t_psum, 2 * g + q - 1)
                nc.vector.tensor_tensor(z1_sb[:, q, :, :].rearrange("p t n -> p (t n)"), z1_bank[q][:, :],
                                        g_sb[:, b, 2 * q:2 * q + 2, :].rearrange("p t n -> p (t n)"),
                                        ALU.add).then_inc(z1_ready, 1)

            def low_pair(g, q):
                dve.wait_ge(h1_hi_ready, 2 * g + q + 1)
                part = slice(q * 2 * P, (q + 1) * 2 * P)
                nc.vector.scalar_tensor_tensor(h1_lo[:, :, part], z1t_bank[:, :].rearrange("p (k e) -> p k e", k=KH),
                                               0.0, h1_hi[:, :, part].bitcast(F32), ALU.max,
                                               ALU.subtract).then_inc(h1_lo_ready, 1)

            def low_messages(g, b):
                dve.wait_ge(m_hi_ready, g + 1)
                nc.vector.tensor_tensor(m_lo[:, b, :, :].rearrange("p t d -> p (t d)"), msg_bank[:, :],
                                        m_hi[:, b, :, :].rearrange("p t d -> p (t d)").bitcast(F32),
                                        ALU.subtract).then_inc(m_lo_ready, 1)

            def incidence(g, t, hot0, first=False):
                if not first:
                    dve.wait_ge(oh_added, GT * g + t)
                nc.vector.tensor_scalar(oh_s[:, :], iota_h[:, :], src_f[:, bass.ds(g * GT + t, 1)], None, ALU.is_equal)
                nc.vector.tensor_scalar(oh_d[:, :], iota_h[:, :], dst_f[:, bass.ds(g * GT + t, 1)], None,
                                        ALU.is_equal).then_inc(oh_made, 1)
                dve.wait_ge(oh_made, GT * g + t + 1)
                if not (first or hot0):
                    dve.wait_ge(inc_ready, GT * g + t - 1)
                nc.vector.tensor_tensor(oh_sum[:, t % 2, :], oh_s[:, :], oh_d[:, :], ALU.add).then_inc(oh_added, 1)

            def group(g, b, n_next, first=False, last=False, last_two=False):
                incidence(g, 0, first, first)
                incidence(g, 1, first)
                if not last:
                    add_gathered(g + 1, 1 - b, 0, n_next)
                    add_gathered(g + 1, 1 - b, 1, n_next)
                    low_pair(g + 1, 0)
                low_messages(g, b)
                if not last:
                    low_pair(g + 1, 1)
                incidence(g, 2, False)
                if not last_two:
                    low_edges(g + 2, b)
                incidence(g, 3, False)

            low_edges(0, 0)
            low_edges(1, 1)
            for q in range(2):
                add_gathered(0, 0, q, 0, first=True)
            for q in range(2):
                low_pair(0, q)
            group(0, 0, 0, first=True)
            with dve.Fori(0, (GROUPS - 4) // 2) as i:
                group(2 * i + 1, 1, i + 1)
                group(2 * i + 2, 0, i + 1)
            half = GROUPS // 2
            group(GROUPS - 3, 1, half - 1)
            group(GROUPS - 2, 0, half - 1, last_two=True)
            group(GROUPS - 1, 1, 0, last=True, last_two=True)

            for k in range(KH * NH):
                m, n = k // NH, k % NH
                dve.wait_ge(u1_psum, k + 1)
                nc.vector.tensor_tensor(uh_sb[:, m, n * HB:(n + 1) * HB], bank[2 + k][:, :],
                                        uh_sb[:, m, n * HB:(n + 1) * HB], ALU.add).then_inc(u1_added, 1)
            dve.wait_ge(u3_psum, NC)
            for k in range(NH):
                step(nc.vector.tensor_tensor(x1_sb[:, 4 * k:4 * k + 4, :].rearrange("p c d -> p (c d)"),
                                             bank[2 + k][:, :],
                                             xb_sb[:, 4 * k:4 * k + 4, :].rearrange("p c d -> p (c d)"), ALU.add))
            settle()
            layer_norm(x1_sb, var2_ready, std2_ready, h2n_ready)
            dve.wait_ge(sqrt_ready, 1)
            for c in range(NC):
                dve.wait_ge(xw_psum, NC)
                nc.vector.tensor_scalar(y_sb[:, c, :], bank[6 + c // 4][:, (c % 4) * D:(c % 4 + 1) * D],
                                        dinv[:, c:c + 1], None, ALU.mult).then_inc(y_ready, 1)
            dve.wait_ge(y_ready, NC)
            for half in range(NH):
                c0, c1 = half * NC // NH, (half + 1) * NC // NH
                dve.wait_ge(agg_psum, c1)
                step(nc.vector.tensor_tensor(o_sb[:, c0:c1, :].rearrange("p c d -> p (c d)"), bank[half][:, :],
                                             y_sb[:, c0:c1, :].rearrange("p c d -> p (c d)"), ALU.add))
                settle()
                for c in range(c0, c1):
                    nc.vector.scalar_tensor_tensor(o_sb[:, c, :], o_sb[:, c, :], dinv[:, c:c + 1], gb_all[:, :],
                                                   ALU.mult, ALU.add).then_inc(pre_ready, 1)
            for half in range(NH):
                c0, c1 = half * NC // NH, (half + 1) * NC // NH
                dve.wait_ge(gelu_ready, half + 1)
                nc.vector.tensor_tensor(o_sb[:, c0:c1, :], o_sb[:, c0:c1, :], x1_sb[:, c0:c1, :],
                                        ALU.add).then_inc(out_ready, 1)


def kernel(**inputs):
    import numpy as np
    import concourse.bacc as bacc
    from concourse.bass_utils import run_bass_kernel_spmd

    a = {k: np.asarray(v) for k, v in inputs.items()}
    tiles = a["src"].shape[0] // P

    def columns(v, n):
        return np.ascontiguousarray(v.reshape(-1, n).T)

    def row(v):
        return np.ascontiguousarray(v.reshape(1, -1))

    L = "L0_gnn_"
    arrays = {
        "x": a["x"],
        "src_cols": columns(a["src"], P),
        "dst_cols": columns(a["dst"], P),
        "edge_attr_t": np.ascontiguousarray(a["edge_attr_64"].T),
        "mW1": a[L + "mW1"], "mb1": row(a[L + "mb1"]),
        "mW2": a[L + "mW2"], "mb2_cols": columns(a[L + "mb2"], P),
        "mW3": a[L + "mW3"], "mb3": a[L + "mb3"],
        "uW1": a[L + "uW1"], "ub1_cols": columns(a[L + "ub1"], P),
        "uW2": a[L + "uW2"], "ub2_cols": columns(a[L + "ub2"], P),
        "uW3": a[L + "uW3"], "ub3": a[L + "ub3"],
        "gcn_W": a["L1_gnn_W"], "gcn_b": a["L1_gnn_b"],
    }
    arrays = {k: np.ascontiguousarray(v) for k, v in arrays.items()}
    nc = bacc.Bacc("TRN2", target_bir_lowering=False, num_devices=1)
    args = [nc.dram_tensor(k, list(v.shape), mybir.dt.from_np(v.dtype), kind="ExternalInput").ap()
            for k, v in arrays.items()]
    out = nc.dram_tensor("out", list(a["x"].shape), F32, kind="ExternalOutput").ap()
    gnn_preln_kernel(nc, *args, out)
    r = run_bass_kernel_spmd(nc, [arrays], core_ids=[0])
    return r.results[0]["out"]
```

```python
from contextlib import ExitStack

import concourse.bass as bass
from concourse import mybir

P = 128
ALU = mybir.AluOpType
ACT = mybir.ActivationFunctionType
F32 = mybir.dt.float32
F32R = mybir.dt.float32r
BF16 = mybir.dt.bfloat16
F16 = mybir.dt.float16
I32 = mybir.dt.int32
AX_X = mybir.AxisListType.X
LN_EPS = 1e-5


def gnn_preln_kernel(nc, x, src_cols, dst_cols, edge_attr_t, mW1, mb1, mW2, mb2_cols, mW3, mb3,
                     uW1, ub1_cols, uW2, ub2_cols, uW3, ub3, gcn_W, gcn_b, out):
    N, D = x.shape
    TILES = src_cols.shape[1]
    ED = edge_attr_t.shape[0]
    H = mW2.shape[0]
    NC = N // P
    KH = H // P
    GT = 4
    GE = GT * P
    GROUPS = TILES // GT
    HB = 512
    NH = N // HB
    PAIR_ATT = 32
    assert D == P and 2 * ED == P and H == 2 * P and GROUPS % 2 == 0

    table_a = nc.dram_tensor("table_a", [N, H], F32).ap()
    table_b = nc.dram_tensor("table_b", [N, H], F32).ap()

    with ExitStack() as ctx:
        def sb(name, shape, dt=F32):
            return ctx.enter_context(nc.sbuf_tensor(name, shape, dt))

        def sem(name):
            return ctx.enter_context(nc.semaphore(name))

        bank = [ctx.enter_context(nc.psum_tensor(f"bank{i}", [P, HB], F32)) for i in range(8)]
        acc_bank = bank[0:2]
        z1_bank = bank[2:4]
        z1t_bank = bank[4]
        z2_bank = bank[5:7]
        msg_bank = bank[7]

        x_sb = sb("x_sb", [P, NC, D])
        ends_i = sb("ends_i", [P, 2, TILES], I32)
        src_i, dst_i = ends_i[:, 0, :], ends_i[:, 1, :]
        w1_sb = sb("w1_sb", [P, 2, H])
        w1e_sb = sb("w1e_sb", [P, H])
        b1_row = sb("b1_row", [1, H])
        w2_sb = sb("w2_sb", [P, KH, H])
        b2_sb = sb("b2_sb", [P, KH])
        w3_sb = sb("w3_sb", [P, KH, D])
        b3_all = sb("b3_all", [P, D])
        u1_sb = sb("u1_sb", [P, 3, H])
        ub1_sb = sb("ub1_sb", [P, KH])
        u2_sb = sb("u2_sb", [P, KH, H])
        ub2_sb = sb("ub2_sb", [P, KH])
        u3_sb = sb("u3_sb", [P, KH, D])
        ub3_all = sb("ub3_all", [P, D])
        gw_sb = sb("gw_sb", [P, D])
        gb_all = sb("gb_all", [P, D])

        iota_f = sb("iota_f", [P, N])
        iota_h = sb("iota_h", [P, N], F16)
        ident = sb("ident", [P, P])
        ones_bf = sb("ones_bf", [P, P], BF16)
        zeros_bf = sb("zeros_bf", [P, HB], BF16)
        ones_row = sb("ones_row", [1, P])

        w1e_hi = sb("w1e_hi", [P, H], F32R)
        w1e_lo = sb("w1e_lo", [P, H], F32R)
        w2_hi = sb("w2_hi", [P, KH, H], F32R)
        w2_lo = sb("w2_lo", [P, KH, H], F32R)

        stats = sb("stats", [P, NC, 6])
        mv = sb("mv", [P, NC, 2])
        std = sb("std", [P, NC])
        rstd = sb("rstd", [P, NC])
        h_sb = sb("h_sb", [P, NC, D])
        h_t = sb("h_t", [P, N])
        att_t = sb("att_t", [P, N])
        tab_sb = sb("tab_sb", [P, NC, 2, H])
        uh_sb = sb("uh_sb", [P, KH, N])
        xb_sb = sb("xb_sb", [P, NC, D])

        src_f = sb("src_f", [P, TILES])
        dst_f = sb("dst_f", [P, TILES])
        neg_mid = sb("neg_mid", [P, TILES])
        half_gap = sb("half_gap", [P, TILES])
        times = sb("times", [P, TILES])
        chunk_i = sb("chunk_i", [P, TILES], I32)
        chunk_f = sb("chunk_f", [P, TILES])
        back_iota = sb("back_iota", [1, GROUPS])
        hi_f = sb("hi_f", [1, NC])
        lo_f = sb("lo_f", [1, NC])
        lo2_f = sb("lo2_f", [1, NC])
        len_f = sb("len_f", [1, NC])
        cum_f = sb("cum_f", [1, NC])
        range_i = sb("range_i", [1, NC, 4], I32)

        oh_src_c = sb("oh_src_c", [P, GT, N], BF16)
        oh_dst_c = sb("oh_dst_c", [P, GT, P], BF16)
        c_sb = sb("c_sb", [P, 2, N])
        ct_sb = sb("ct_sb", [P, NC, N])
        deg_in2 = sb("deg_in2", [P, NC, NH])
        deg_in = sb("deg_in", [P, NC])
        deg_out = sb("deg_out", [P, NC])
        cnt = sb("cnt", [P, NC])
        dinv = sb("dinv", [P, NC])
        cb3 = sb("cb3", [P, NC, D])

        gidx = sb("gidx", [P, 4, 2, 2], I32)
        g_sb = sb("g_sb", [P, 2, GT, H])
        e_raw = sb("e_raw", [P, 2, GE])
        e_hl = sb("e_hl", [P, 2, GE], F32R)
        z1_sb = sb("z1_sb", [P, 2, 2, H])
        h1_hi = sb("h1_hi", [P, 2, KH, GE], F32R)
        h1_lo = sb("h1_lo", [P, 2, KH, GE], F32R)
        h2_sb = sb("h2_sb", [P, KH, GE])
        m_hi = sb("m_hi", [P, 2, GT, D], F32R)
        m_lo = sb("m_lo", [P, 2, GT, D], F32R)
        inc = sb("inc", [P, GT, N], F32R)

        dist = oh_src_c[:, :, :].rearrange("p t n -> p (t n)").bitcast(F16).rearrange("p (t n) -> p t n", t=GT)
        spare = z1_sb[:, :, :, :].rearrange("p q t n -> p (q t n)")
        grp = z1_sb[0:1, 0, :, :].rearrange("p t n -> p (t n)").rearrange("p (c g) -> p c g", c=NC)
        grp_w = z1_sb[0:1, 1, :, :].rearrange("p t n -> p (t n)").rearrange("p (c g) -> p c g", c=NC)
        in_chunk = g_sb[:, 0, :, :].rearrange("p t n -> p (t n)").bitcast(BF16).rearrange("p (c t) -> p c t", c=NC)
        tab_all = tab_sb[:, :, :, :].rearrange("p c t n -> p (c t n)")
        u_a = tab_all[:, 0:KH * N].rearrange("p (k n) -> p k n", k=KH)
        sum_t = tab_all[:, KH * N:KH * N + N]
        x1_sb = tab_all[:, KH * N + N:KH * N + 2 * N].rearrange("p (c d) -> p c d", c=NC)
        y_sb = c_sb[:, 0, :].rearrange("p (c d) -> p c d", c=NC)
        o_sb = c_sb[:, 1, :].rearrange("p (c d) -> p c d", c=NC)

        ld_x = sem("ld_x")
        ld_idx = sem("ld_idx")
        ld_w = sem("ld_w")
        consts_pool = sem("consts_pool")
        pool_step = sem("pool_step")
        dve_step = sem("dve_step")
        var_ready = sem("var_ready")
        std_ready = sem("std_ready")
        h_ready = sem("h_ready")
        ht_psum = sem("ht_psum")
        ht_ready = sem("ht_ready")
        att_ready = sem("att_ready")
        tab_psum = sem("tab_psum")
        tab_ready = sem("tab_ready")
        tab_stored = sem("tab_stored")
        uh_psum = sem("uh_psum")
        uh_ready = sem("uh_ready")
        chunks_marked = sem("chunks_marked")
        marks_psum = sem("marks_psum")
        ranges_ready = sem("ranges_ready")
        ends_ready = sem("ends_ready")
        split_ready = sem("split_ready")
        c_hot = sem("c_hot")
        c_used = sem("c_used")
        c_psum = sem("c_psum")
        c_ready = sem("c_ready")
        ct_psum = sem("ct_psum")
        ct_ready = sem("ct_ready")
        degs_ready = sem("degs_ready")
        sqrt_ready = sem("sqrt_ready")
        cb3_ready = sem("cb3_ready")
        gidx_ready = sem("gidx_ready")
        ga_done = [[sem(f"ga_done{b}_{j}") for j in range(GT)] for b in range(2)]
        gb_done = [[sem(f"gb_done{b}_{j}") for j in range(GT)] for b in range(2)]
        e_loaded = [sem("e_loaded0"), sem("e_loaded1")]
        e_cast = sem("e_cast")
        e_ready = sem("e_ready")
        z1_psum = sem("z1_psum")
        z1_ready = sem("z1_ready")
        z1t_psum = sem("z1t_psum")
        h1_hi_ready = sem("h1_hi_ready")
        h1_lo_ready = sem("h1_lo_ready")
        z2_psum = sem("z2_psum")
        h2_ready = sem("h2_ready")
        m_psum = sem("m_psum")
        m_hi_ready = sem("m_hi_ready")
        m_lo_ready = sem("m_lo_ready")
        dist_ready = sem("dist_ready")
        inc_ready = sem("inc_ready")
        scattered = sem("scattered")
        sum_ready = sem("sum_ready")
        u1_psum = sem("u1_psum")
        u1_added = sem("u1_added")
        u1_ready = sem("u1_ready")
        u2_psum = sem("u2_psum")
        u2_ready = sem("u2_ready")
        u3_psum = sem("u3_psum")
        x1_ready = sem("x1_ready")
        var2_ready = sem("var2_ready")
        std2_ready = sem("std2_ready")
        h2n_ready = sem("h2n_ready")
        h2t_psum = sem("h2t_psum")
        h2t_ready = sem("h2t_ready")
        xw_psum = sem("xw_psum")
        y_ready = sem("y_ready")
        agg_psum = sem("agg_psum")
        pre_ready = sem("pre_ready")
        gelu_ready = sem("gelu_ready")
        out_ready = sem("out_ready")
        stored = sem("stored")

        block = ctx.enter_context(nc.Block())

        def exists(g):
            return not isinstance(g, int) or 0 <= g < GROUPS

        def wait(engine, semaphore, value):
            if not isinstance(value, int) or value > 0:
                engine.wait_ge(semaphore, value)

        def run_groups(engine, group):
            for g in range(-3, 2):
                group(g, g % 2, g // 2)
            with engine.Fori(1, GROUPS // 2 - 2) as i:
                for b in range(2):
                    group(2 * i + b, b, i)
            for g in range(GROUPS - 4, GROUPS + 1):
                group(g, g % 2, g // 2)

        @block.sync
        def _(sp):
            sp.dma_start(x_sb[:, :, :], x.rearrange("(c p) d -> p c d", p=P)).then_inc(ld_x, 16)
            sp.dma_start(dst_i, dst_cols).then_inc(ld_idx, 16)
            sp.dma_start(src_i, src_cols).then_inc(ld_idx, 16)
            loads = [
                (w1_sb[:, :, :], mW1[0:2 * D, :].rearrange("(k p) n -> p k n", p=P)),
                (b1_row[:, :], mb1),
                (w1e_sb[0:ED, :], mW1[2 * D:2 * D + ED, :]),
                (w1e_sb[ED:P, :], mW1[2 * D:2 * D + ED, :]),
                (u1_sb[:, :, :], uW1.rearrange("(k p) n -> p k n", p=P)),
                (ub1_sb[:, :], ub1_cols),
                (w2_sb[:, :, :], mW2.rearrange("(k p) n -> p k n", p=P)),
                (b2_sb[:, :], mb2_cols),
                (w3_sb[:, :, :], mW3.rearrange("(k p) n -> p k n", p=P)),
                (b3_all[:, :], mb3.partition_broadcast(P)),
                (u2_sb[:, :, :], uW2.rearrange("(k p) n -> p k n", p=P)),
                (ub2_sb[:, :], ub2_cols),
                (u3_sb[:, :, :], uW3.rearrange("(k p) n -> p k n", p=P)),
                (ub3_all[:, :], ub3.partition_broadcast(P)),
                (gw_sb[:, :], gcn_W),
                (gb_all[:, :], gcn_b.partition_broadcast(P)),
            ]
            for to, frm in loads:
                sp.dma_start(to, frm).then_inc(ld_w, 16)

            def load_edges(g, b):
                cols = edge_attr_t[:, bass.ds(g * GE, GE)]
                sp.dma_start(e_raw[0:ED, b, :], cols).then_inc(e_loaded[b], 16)
                sp.dma_start(e_raw[ED:P, b, :], cols).then_inc(e_loaded[b], 16)

            load_edges(0, 0)
            load_edges(1, 1)
            sp.wait_ge(tab_ready, NC)
            sp.dma_start(table_a.rearrange("(c p) n -> p c n", p=P), tab_sb[:, :, 0, :]).then_inc(tab_stored, 16)
            sp.dma_start(table_b.rearrange("(c p) n -> p c n", p=P), tab_sb[:, :, 1, :]).then_inc(tab_stored, 16)
            with sp.Fori(0, GROUPS // 2 - 1) as i:
                for b in range(2):
                    sp.wait_ge(e_ready, 2 * i + b + 1)
                    load_edges(2 * i + b + 2, b)
            for half in range(NH):
                sp.wait_ge(out_ready, half + 1)
                c0, c1 = half * NC // NH, (half + 1) * NC // NH
                sp.dma_start(out[c0 * P:c1 * P, :].rearrange("(c p) d -> p c d", p=P),
                             o_sb[:, c0:c1, :]).then_inc(stored, 16)
            sp.wait_ge(stored, 16 * NH)

        @block.gpsimd
        def _(pool):
            steps = [0]

            def step(ins):
                steps[0] += 1
                ins.then_inc(pool_step, 1)
                pool.wait_ge(pool_step, steps[0])

            nc.gpsimd.iota(iota_f[:, :], pattern=[[1, N]], base=0, channel_multiplier=0,
                           allow_small_or_imprecise_dtypes=True).then_inc(consts_pool, 1)
            nc.gpsimd.memset(ones_bf[:, :], 1.0).then_inc(consts_pool, 1)
            nc.gpsimd.memset(zeros_bf[:, :], 0.0).then_inc(consts_pool, 1)
            nc.gpsimd.memset(ones_row[:, :], 1.0).then_inc(consts_pool, 1)
            nc.gpsimd.iota(back_iota[:, :], pattern=[[-1, GROUPS]], base=GROUPS, channel_multiplier=0,
                           allow_small_or_imprecise_dtypes=True).then_inc(consts_pool, 1)
            step(nc.gpsimd.memset(ident[:, :], 0.0))
            nc.gpsimd.affine_select(out=ident[:, :], in_=ident[:, :], compare_op=ALU.not_equal, fill=1.0,
                                    base=0, pattern=[[-1, P]], channel_multiplier=1).then_inc(consts_pool, 1)
            pool.wait_ge(ld_idx, 32)

            def gather_src(p, s, n):
                b, q = s // 2, s % 2
                wait(pool, z1_ready, p - 3)
                copied = p + 1
                if not isinstance(p, int):
                    copied = pool.to_reg(copied)
                nc.gpsimd.tensor_copy(gidx[:, s, :, :], ends_i[:, :, bass.ds(p * 2, 2)]).then_inc(gidx_ready, 1)
                pool.wait_ge(tab_stored, 32)
                pool.wait_ge(gidx_ready, copied)
                for t in range(2):
                    j = 2 * q + t
                    nc.gpsimd.indirect_dma_start(
                        g_sb[:, b, j, :], None, table_a,
                        bass.IndirectOffsetOnAxis(ap=gidx[:, s, 0, t:t + 1], axis=0),
                    ).then_inc(ga_done[b][j], 16)

            def gather_dst(p, s, n):
                b, q = s // 2, s % 2
                landed = 16 * (n + 1)
                if not isinstance(p, int):
                    landed = pool.to_reg(landed)
                for t in range(2):
                    j = 2 * q + t
                    pool.wait_ge(tab_stored, 32)
                    pool.wait_ge(ga_done[b][j], landed)
                    nc.gpsimd.indirect_dma_start(
                        g_sb[:, b, j, :], None, table_b,
                        bass.IndirectOffsetOnAxis(ap=gidx[:, s, 1, t:t + 1], axis=0), compute_op=ALU.add,
                    ).then_inc(gb_done[b][j], 16)

            def gather_step(p, s, n):
                if not isinstance(p, int) or p + 1 < 2 * GROUPS:
                    gather_src(p + 1, (s + 1) % 4, n + (s + 1) // 4)
                gather_dst(p, s, n)

            gather_src(0, 0, 0)
            for s in range(4):
                gather_step(s, s, 0)
            with pool.Fori(1, GROUPS // 2 - 1) as i:
                for s in range(4):
                    gather_step(4 * i + s, s, i)
            for s in range(4):
                gather_step(2 * GROUPS - 4 + s, s, GROUPS // 2 - 1)

        @block.tensor
        def _(pe):
            pe.wait_ge(consts_pool, 6)
            pe.wait_ge(chunks_marked, 1)
            marks = in_chunk.rearrange("p c t -> p (c t)")
            for q in range(4):
                mm = nc.tensor.matmul(bank[4 + q][0:1, :], ones_bf[:, 0:1], marks[:, q * HB:(q + 1) * HB],
                                      start=True, stop=True)
            mm.then_inc(marks_psum, 1)
            pe.wait_ge(h_ready, 1)
            for c in range(NC):
                mm = nc.tensor.transpose(bank[c // 4][:, (c % 4) * P:(c % 4 + 1) * P], h_sb[:, c, :], ident[:, :])
            mm.then_inc(ht_psum, 1)
            pe.wait_ge(ht_ready, 1)
            pe.wait_ge(ld_w, 16 * 16)
            for c in range(NC):
                if c >= 2:
                    pe.wait_ge(tab_ready, c - 1)
                to = bank[2 + c % 2]
                hc = h_t[:, c * P:(c + 1) * P]
                nc.tensor.matmul(to[:, 0:H], hc, w1_sb[:, 0, :], start=True, stop=False, skip_group_check=True)
                nc.tensor.matmul(to[:, 0:H], ones_row[:, :], b1_row[:, :], start=False, stop=True,
                                 skip_group_check=True)
                nc.tensor.matmul(to[:, H:2 * H], hc, w1_sb[:, 1, :], start=False, stop=True,
                                 skip_group_check=True).then_inc(tab_psum, 1)
            pe.wait_ge(att_ready, 1)
            for k in range(KH * NH):
                m, n = k // NH, k % NH
                if k >= 2:
                    pe.wait_ge(uh_ready, k - 1)
                to = bank[k % 2]
                nc.tensor.matmul(to[:, :], u1_sb[:, 0, m * P:(m + 1) * P], h_t[:, n * HB:(n + 1) * HB],
                                 start=True, stop=False)
                nc.tensor.matmul(to[:, :], u1_sb[:, 2, m * P:(m + 1) * P], att_t[:, n * HB:(n + 1) * HB],
                                 start=False, stop=True).then_inc(uh_psum, 1)
            pe.wait_ge(uh_ready, KH * NH)
            pe.wait_ge(tab_ready, NC)
            pe.wait_ge(ranges_ready, 1)
            for c in range(NC):
                first_visit = pe.value_load(range_i[0:1, c, 0:1], min_val=0, max_val=NC * GROUPS)
                end_visit = pe.value_load(range_i[0:1, c, 1:2], min_val=1, max_val=NC * GROUPS)
                cb = bank[2 * (c % 2):2 * (c % 2) + 2]
                if c >= 2:
                    pe.wait_ge(c_ready, c - 1)
                for n in range(NH):
                    nc.tensor.matmul(cb[n][:, :], zeros_bf[:, 0:P], zeros_bf[:, :], start=True, stop=False,
                                     skip_group_check=True)
                with pe.Fori(first_visit, end_visit) as visit:
                    for j in range(GT):
                        pe.wait_ge(c_hot, visit * GT + (j + 1))
                        for n in range(NH):
                            mm = nc.tensor.matmul(cb[n][:, :], oh_dst_c[:, j, :],
                                                  oh_src_c[:, j, n * HB:(n + 1) * HB],
                                                  start=False, stop=False, skip_group_check=True)
                        mm.then_inc(c_used, 1)
                for n in range(NH):
                    mm = nc.tensor.matmul(cb[n][:, :], zeros_bf[:, 0:P], zeros_bf[:, :], start=False, stop=True,
                                          skip_group_check=True)
                mm.then_inc(c_psum, 1)
                for cc in ([c - 1] if c else []) + ([c] if c == NC - 1 else []):
                    pe.wait_ge(c_ready, cc + 1)
                    if cc:
                        pe.wait_ge(ct_ready, cc)
                    for s in range(NC):
                        mm = nc.tensor.transpose(bank[4 + s // 4][:, (s % 4) * P:(s % 4 + 1) * P],
                                                 c_sb[:, cc % 2, s * P:(s + 1) * P], ident[:, :])
                    mm.then_inc(ct_psum, 1)

            pe.wait_ge(cb3_ready, 1)
            pe.wait_ge(ct_ready, NC)
            for c in range(NC):
                nc.tensor.matmul(acc_bank[c // 4][:, (c % 4) * P:(c % 4 + 1) * P], cb3[:, c, :], ident[:, :],
                                 start=(c % 4 == 0), stop=False, skip_group_check=True)
            pe.wait_ge(split_ready, 1)

            def first_layer(g, b, q):
                if q == 0:
                    pe.wait_ge(e_ready, g + 1)
                for t in range(2):
                    ee = e_hl[:, b, (2 * q + t) * P:(2 * q + t + 1) * P]
                    to = z1_bank[q][:, t * H:(t + 1) * H]
                    nc.tensor.matmul(to, ee, w1e_hi[:, :], start=(t == 0), stop=False, skip_group_check=True)
                    mm = nc.tensor.matmul(to, ee, w1e_lo[:, :], start=False, stop=True, skip_group_check=True)
                mm.then_inc(z1_psum, 1)

            def transpose_pair(g, q):
                wait(pe, z1_ready, 2 * g + q + 1)
                wait(pe, h1_lo_ready, 2 * g + q)
                for k in range(KH):
                    for t in range(2):
                        mm = nc.tensor.transpose(z1t_bank[:, (2 * k + t) * P:(2 * k + t + 1) * P],
                                                 z1_sb[:, q, t, k * P:(k + 1) * P], ident[:, :])
                mm.then_inc(z1t_psum, 1)

            def second_layer(g, b, m):
                if m == 0:
                    pe.wait_ge(h1_lo_ready, 2 * g + 2)
                wait(pe, h2_ready, 2 * g + m - 1)
                parts = [(w, a, k) for w, a in ((w2_hi, h1_hi), (w2_lo, h1_hi), (w2_hi, h1_lo)) for k in range(KH)]
                for n, (w, a, k) in enumerate(parts):
                    mm = nc.tensor.matmul(z2_bank[m][:, :], w[:, k, m * P:(m + 1) * P], a[:, b, k, :],
                                          start=(n == 0), stop=(n == len(parts) - 1))
                mm.then_inc(z2_psum, 1)

            def messages(g, tiles):
                if tiles[0] == 0:
                    pe.wait_ge(h2_ready, 2 * g + 2)
                    wait(pe, m_lo_ready, g)
                for t in tiles:
                    for k in range(KH):
                        mm = nc.tensor.matmul(msg_bank[:, t * D:(t + 1) * D], h2_sb[:, k, t * P:(t + 1) * P],
                                              w3_sb[:, k, :], start=(t == 0 and k == 0), stop=(k == KH - 1),
                                              skip_group_check=True)
                mm.then_inc(m_psum, 1)

            def scatter(g, b, t):
                if t == 0:
                    pe.wait_ge(m_lo_ready, g + 1)
                pe.wait_ge(inc_ready, GT * g + (t + 1))
                for part in (m_hi, m_lo):
                    for n in range(NH):
                        mm = nc.tensor.matmul(acc_bank[n][:, :], part[:, b, t, :], inc[:, t, n * HB:(n + 1) * HB],
                                              start=False, stop=False, skip_group_check=True)
                mm.then_inc(scattered, 1)

            def group(g, b, i):
                now, nxt, ahead, past = exists(g), exists(g + 1), exists(g + 2), exists(g - 1)
                if now:
                    second_layer(g, b, 0)
                if nxt:
                    transpose_pair(g + 1, 0)
                if now:
                    second_layer(g, b, 1)
                if past:
                    scatter(g - 1, 1 - b, 0)
                if nxt:
                    transpose_pair(g + 1, 1)
                if past:
                    scatter(g - 1, 1 - b, 1)
                if now:
                    messages(g, (0, 1))
                if ahead:
                    first_layer(g + 2, b, 0)
                if now:
                    messages(g, (2, 3))
                if ahead:
                    first_layer(g + 2, b, 1)
                if past:
                    scatter(g - 1, 1 - b, 2)
                    scatter(g - 1, 1 - b, 3)

            run_groups(pe, group)

            for k in range(KH * NH):
                m, n = k // NH, k % NH
                if m == 0:
                    pe.wait_ge(sum_ready, n + 1)
                nc.tensor.matmul(bank[2 + k][:, :], u1_sb[:, 1, m * P:(m + 1) * P], sum_t[:, n * HB:(n + 1) * HB],
                                 start=True, stop=True).then_inc(u1_psum, 1)
            u2_bank = [bank[0], bank[1], bank[6], bank[7]]
            pe.wait_ge(u1_ready, KH * NH)
            for k in range(KH * NH):
                m, n = k // NH, k % NH
                for kk in range(KH):
                    mm = nc.tensor.matmul(u2_bank[k][:, :], u2_sb[:, kk, m * P:(m + 1) * P],
                                          uh_sb[:, kk, n * HB:(n + 1) * HB], start=(kk == 0), stop=(kk == KH - 1))
                mm.then_inc(u2_psum, 1)
            pe.wait_ge(u2_ready, KH * NH)
            for c in range(NC):
                for kk in range(KH):
                    mm = nc.tensor.matmul(bank[2 + c // 4][:, (c % 4) * D:(c % 4 + 1) * D],
                                          u_a[:, kk, c * P:(c + 1) * P], u3_sb[:, kk, :],
                                          start=(kk == 0 and c % 4 == 0), stop=(kk == KH - 1), skip_group_check=True)
                mm.then_inc(u3_psum, 1)
            pe.wait_ge(h2n_ready, 1)
            for c in range(NC):
                mm = nc.tensor.transpose(bank[4 + c // 4][:, (c % 4) * P:(c % 4 + 1) * P], h_sb[:, c, :], ident[:, :])
            mm.then_inc(h2t_psum, 1)
            pe.wait_ge(h2t_ready, 1)
            for c in range(NC):
                mm = nc.tensor.matmul(bank[6 + c // 4][:, (c % 4) * D:(c % 4 + 1) * D], h_t[:, c * P:(c + 1) * P],
                                      gw_sb[:, :], start=(c % 4 == 0), stop=True, skip_group_check=True)
                mm.then_inc(xw_psum, 1)
            pe.wait_ge(y_ready, NC)
            for c in range(NC):
                for s in range(NC):
                    mm = nc.tensor.matmul(bank[c // 4][:, (c % 4) * D:(c % 4 + 1) * D],
                                          ct_sb[:, s, c * P:(c + 1) * P], y_sb[:, s, :],
                                          start=(s == 0 and c % 4 == 0), stop=(s == NC - 1), skip_group_check=True)
                mm.then_inc(agg_psum, 1)

        @block.scalar
        def _(act):
            act.wait_ge(var_ready, 1)
            nc.scalar.activation(std[:, :], std[:, :], ACT.Sqrt).then_inc(std_ready, 1)
            act.wait_ge(ht_psum, 1)
            nc.scalar.copy(h_t[:, 0:HB], bank[0][:, :])
            nc.scalar.copy(h_t[:, HB:N], bank[1][:, :]).then_inc(ht_ready, 1)
            for c in range(NC):
                act.wait_ge(tab_psum, c + 1)
                nc.scalar.copy(tab_sb[:, c, :, :].rearrange("p t n -> p (t n)"), bank[2 + c % 2][:, :]).then_inc(tab_ready, 1)
            for k in range(KH * NH):
                m, n = k // NH, k % NH
                act.wait_ge(uh_psum, k + 1)
                nc.scalar.activation(uh_sb[:, m, n * HB:(n + 1) * HB], bank[k % 2][:, :], ACT.Identity,
                                     bias=ub1_sb[:, m:m + 1]).then_inc(uh_ready, 1)

            for c in range(NC):
                act.wait_ge(c_psum, c + 1)
                if c >= 2:
                    act.wait_ge(ct_psum, c - 1)
                for n in range(NH):
                    cp = nc.scalar.activation(c_sb[:, c % 2, n * HB:(n + 1) * HB], bank[2 * (c % 2) + n][:, :],
                                              ACT.Copy, accum_out=deg_in2[:, c, n:n + 1])
                cp.then_inc(c_ready, 1)
                if c:
                    for n in range(NH):
                        if n == 0:
                            act.wait_ge(ct_psum, c)
                        cp = nc.scalar.copy(ct_sb[:, 4 * n:4 * n + 4, (c - 1) * P:c * P],
                                            bank[4 + n][:, :].rearrange("p (s d) -> p s d", s=4))
                    cp.then_inc(ct_ready, 1)
            act.wait_ge(ct_psum, NC)
            for n in range(NH):
                cp = nc.scalar.copy(ct_sb[:, 4 * n:4 * n + 4, (NC - 1) * P:NC * P],
                                    bank[4 + n][:, :].rearrange("p (s d) -> p s d", s=4))
            cp.then_inc(ct_ready, 1)
            act.wait_ge(ct_ready, NC)
            for s in range(NC):
                if s:
                    act.wait_ge(degs_ready, s)
                nc.scalar.activation(spare, ct_sb[:, s, :], ACT.Copy, accum_out=deg_out[:, s:s + 1]).then_inc(degs_ready, 1)
            act.wait_ge(cb3_ready, 1)
            nc.scalar.activation(dinv[:, :], dinv[:, :], ACT.Sqrt).then_inc(sqrt_ready, 1)

            def split_edges(g, b, n):
                act.wait_ge(e_loaded[b], 32 * (n + 1))
                wait(act, z1_psum, 2 * (g - 1))
                nc.scalar.copy(e_hl[:, b, :], e_raw[:, b, :]).then_inc(e_cast, 1)

            def relu_pair(g, b, q):
                act.wait_ge(z1t_psum, 2 * g + q + 1)
                wait(act, z2_psum, 2 * g - 2)
                nc.scalar.activation(h1_hi[:, b, :, q * 2 * P:(q + 1) * 2 * P],
                                     z1t_bank[:, :].rearrange("p (k e) -> p k e", k=KH), ACT.Relu).then_inc(h1_hi_ready, 1)

            def relu_second(g, m):
                act.wait_ge(z2_psum, 2 * g + m + 1)
                wait(act, m_psum, 2 * g)
                nc.scalar.activation(h2_sb[:, m, :], z2_bank[m][:, :], ACT.Relu, bias=b2_sb[:, m:m + 1]).then_inc(h2_ready, 1)

            def distance(g, t):
                wait(act, inc_ready, GT * g + (t - 3))
                nc.scalar.activation(dist[:, t, :], iota_h[:, :], ACT.Abs,
                                     bias=neg_mid[:, bass.ds(g * GT + t, 1)]).then_inc(dist_ready, 1)

            def high_messages(g, b):
                act.wait_ge(m_psum, 2 * g + 2)
                wait(act, scattered, GT * (g - 1))
                nc.scalar.copy(m_hi[:, b, :, :].rearrange("p t d -> p (t d)"), msg_bank[:, :]).then_inc(m_hi_ready, 1)

            def group(g, b, i):
                now, nxt = exists(g), exists(g + 1)
                if now:
                    relu_second(g, 0)
                if nxt:
                    relu_pair(g + 1, 1 - b, 0)
                if now:
                    relu_second(g, 1)
                    distance(g, 1)
                if nxt:
                    relu_pair(g + 1, 1 - b, 1)
                if exists(g + 3):
                    split_edges(g + 3, 1 - b, i + 1 + b)
                if now:
                    distance(g, 2)
                    high_messages(g, b)
                    distance(g, 3)
                if nxt:
                    distance(g + 1, 0)

            run_groups(act, group)

            for n in range(NH):
                act.wait_ge(scattered, GT * GROUPS)
                nc.scalar.copy(sum_t[:, n * HB:(n + 1) * HB], acc_bank[n][:, :]).then_inc(sum_ready, 1)
            for k in range(KH * NH):
                m, n = k // NH, k % NH
                act.wait_ge(u1_added, k + 1)
                nc.scalar.activation(uh_sb[:, m, n * HB:(n + 1) * HB], uh_sb[:, m, n * HB:(n + 1) * HB],
                                     ACT.Relu).then_inc(u1_ready, 1)
            u2_bank = [bank[0], bank[1], bank[6], bank[7]]
            for k in range(KH * NH):
                m, n = k // NH, k % NH
                act.wait_ge(u2_psum, k + 1)
                nc.scalar.activation(u_a[:, m, n * HB:(n + 1) * HB], u2_bank[k][:, :], ACT.Relu,
                                     bias=ub2_sb[:, m:m + 1]).then_inc(u2_ready, 1)
            act.wait_ge(var2_ready, 1)
            nc.scalar.activation(std[:, :], std[:, :], ACT.Sqrt).then_inc(std2_ready, 1)
            act.wait_ge(h2t_psum, 1)
            nc.scalar.copy(h_t[:, 0:HB], bank[4][:, :])
            nc.scalar.copy(h_t[:, HB:N], bank[5][:, :]).then_inc(h2t_ready, 1)
            for half in range(NH):
                c0, c1 = half * NC // NH, (half + 1) * NC // NH
                act.wait_ge(pre_ready, c1)
                nc.scalar.activation(o_sb[:, c0:c1, :], o_sb[:, c0:c1, :], ACT.Gelu).then_inc(gelu_ready, 1)

        @block.vector
        def _(dve):
            steps = [0]

            def step(ins):
                steps[0] += 1
                ins.then_inc(dve_step, 1)

            def settle():
                dve.wait_ge(dve_step, steps[0])

            def layer_norm(rows, ready, done, final):
                for c in range(NC):
                    step(nc.vector.bn_stats(stats[:, c, :], rows[:, c, :]))
                settle()
                for c in range(NC):
                    step(nc.vector.bn_aggr(mv[:, c, :], stats[:, c, :]))
                settle()
                nc.vector.tensor_scalar(std[:, :], mv[:, :, 1], LN_EPS, None, ALU.add).then_inc(ready, 1)
                for c in range(NC):
                    step(nc.vector.tensor_scalar(h_sb[:, c, :], rows[:, c, :], mv[:, c, 0:1], 0.0,
                                                 ALU.subtract, ALU.max))
                dve.wait_ge(done, 1)
                step(nc.vector.reciprocal(rstd[:, :], std[:, :]))
                settle()
                for c in range(NC):
                    hh = nc.vector.tensor_scalar(h_sb[:, c, :], h_sb[:, c, :], rstd[:, c:c + 1], None, ALU.mult)
                hh.then_inc(final, 1)

            dve.wait_ge(ld_idx, 32)
            step(nc.vector.tensor_scalar(chunk_i[:, :], dst_i, 7, None, ALU.arith_shift_right))
            nc.vector.tensor_copy(src_f[:, :], src_i).then_inc(ends_ready, 1)
            nc.vector.tensor_copy(dst_f[:, :], dst_i).then_inc(ends_ready, 1)
            settle()
            step(nc.vector.tensor_copy(chunk_f[:, :], chunk_i[:, :]))
            settle()
            for c in range(NC):
                mark = nc.vector.tensor_scalar(in_chunk[:, c, :], chunk_f[:, :], float(c), None, ALU.is_equal)
            mark.then_inc(chunks_marked, 1)
            dve.wait_ge(ld_x, 16)
            layer_norm(x_sb, var_ready, std_ready, h_ready)
            dve.wait_ge(marks_psum, 1)
            dve.wait_ge(consts_pool, 6)
            per_bank = HB // TILES
            for q in range(4):
                step(nc.vector.tensor_reduce(grp[:, per_bank * q:per_bank * (q + 1), :],
                                             bank[4 + q][0:1, :].rearrange("p (c g t) -> p c g t", c=per_bank, t=GT),
                                             AX_X, ALU.max))
            settle()
            step(nc.vector.tensor_scalar(grp[:, :, :], grp[:, :, :], 1.0, None, ALU.min))
            settle()
            step(nc.vector.tensor_tensor(grp_w[:, :, :], grp[:, :, :],
                                         back_iota[:, :].unsqueeze(1).broadcast_to([1, NC, GROUPS]), ALU.mult))
            settle()
            step(nc.vector.tensor_reduce(lo_f[:, :], grp_w[:, :, :], AX_X, ALU.max))
            settle()
            step(nc.vector.tensor_tensor(grp_w[:, :, :], grp[:, :, :],
                                         iota_f[0:1, 1:GROUPS + 1].unsqueeze(1).broadcast_to([1, NC, GROUPS]), ALU.mult))
            settle()
            step(nc.vector.tensor_reduce(hi_f[:, :], grp_w[:, :, :], AX_X, ALU.max))
            settle()
            step(nc.vector.tensor_scalar(hi_f[:, :], hi_f[:, :], 1.0, None, ALU.max))
            step(nc.vector.tensor_scalar(lo_f[:, :], lo_f[:, :], -1.0, float(GROUPS), ALU.mult, ALU.add))
            settle()
            step(nc.vector.tensor_scalar(len_f[:, :], hi_f[:, :], -1.0, None, ALU.add))
            settle()
            step(nc.vector.tensor_tensor(lo2_f[:, :], lo_f[:, :], len_f[:, :], ALU.min))
            settle()
            step(nc.vector.tensor_tensor(len_f[:, :], hi_f[:, :], lo2_f[:, :], ALU.subtract))
            step(nc.vector.memset(cum_f[:, 0:1], 0.0))
            settle()
            for c in range(1, NC):
                step(nc.vector.tensor_tensor(cum_f[:, c:c + 1], cum_f[:, c - 1:c], len_f[:, c - 1:c], ALU.add))
                settle()
            step(nc.vector.tensor_tensor(hi_f[:, :], cum_f[:, :], len_f[:, :], ALU.add))
            step(nc.vector.tensor_tensor(lo_f[:, :], lo2_f[:, :], cum_f[:, :], ALU.subtract))
            settle()
            step(nc.vector.tensor_copy(range_i[:, :, 0], cum_f[:, :]))
            step(nc.vector.tensor_copy(range_i[:, :, 1], hi_f[:, :]))
            step(nc.vector.tensor_copy(range_i[:, :, 2], lo_f[:, :]))
            settle()
            step(nc.vector.tensor_copy(iota_h[:, :], iota_f[:, :]))
            dve.wait_ge(ht_ready, 1)
            h_pair = h_t[:, :].rearrange("p (b a n) -> p b a n", a=2, n=PAIR_ATT)
            a_pair = att_t[:, :].rearrange("p (b a n) -> p b a n", a=2, n=PAIR_ATT)
            for a in range(2):
                at = nc.vector.tensor_tensor(a_pair[:, :, a, :], h_pair[:, :, a, :], h_pair[:, :, 1 - a, :], ALU.subtract)
            at.then_inc(att_ready, 1)
            dve.wait_ge(ld_w, 16 * 16)
            step(nc.vector.tensor_copy(w1e_hi[:, :], w1e_sb[:, :]))
            step(nc.vector.tensor_copy(w2_hi[:, :, :], w2_sb[:, :, :]))
            settle()
            nc.vector.tensor_tensor(w1e_lo[:, :], w1e_sb[:, :], w1e_hi[:, :].bitcast(F32), ALU.subtract)
            nc.vector.tensor_tensor(w2_lo[:, :, :], w2_sb[:, :, :], w2_hi[:, :, :].bitcast(F32),
                                    ALU.subtract).then_inc(split_ready, 1)
            step(nc.vector.tensor_tensor(xb_sb[:, :, :], x_sb[:, :, :],
                                         ub3_all[:, :].unsqueeze(1).broadcast_to([P, NC, D]), ALU.add))
            dve.wait_ge(ends_ready, 2)
            settle()
            nc.vector.tensor_copy(range_i[:, :, 3], hi_f[:, :]).then_inc(ranges_ready, 1)
            dve.wait_ge(ranges_ready, 1)
            for c in range(NC):
                first_visit = dve.value_load(range_i[0:1, c, 0:1], min_val=0, max_val=NC * GROUPS)
                end_visit = dve.value_load(range_i[0:1, c, 1:2], min_val=1, max_val=NC * GROUPS)
                shift = dve.value_load(range_i[0:1, c, 2:3], min_val=-NC * GROUPS, max_val=GROUPS)
                if c == 0:
                    for j in range(GT):
                        nc.vector.memset(oh_dst_c[:, j, :], 0.0).then_inc(c_used, 1)
                with dve.Fori(first_visit, end_visit) as visit:
                    group_no = nc.s_assert_within(
                        visit + shift, 0, GROUPS - 1,
                        skip_runtime_bounds_check_because="visits of a chunk run over its range of groups")
                    tile0 = group_no * GT
                    for j in range(GT):
                        dve.wait_ge(c_used, visit * GT + (j + 1))
                        nc.vector.tensor_scalar(oh_dst_c[:, j, :], iota_h[:, c * P:(c + 1) * P],
                                                dst_f[:, bass.ds(tile0 + j, 1)], None, ALU.is_equal)
                        nc.vector.tensor_scalar(oh_src_c[:, j, :], iota_h[:, :],
                                                src_f[:, bass.ds(tile0 + j, 1)], None,
                                                ALU.is_equal).then_inc(c_hot, 1)
            step(nc.vector.tensor_tensor(neg_mid[:, :], src_f[:, :], dst_f[:, :], ALU.add))
            step(nc.vector.tensor_tensor(half_gap[:, :], src_f[:, :], dst_f[:, :], ALU.subtract))
            step(nc.vector.tensor_tensor(times[:, :], src_f[:, :], dst_f[:, :], ALU.is_equal))
            settle()
            step(nc.vector.tensor_scalar(neg_mid[:, :], neg_mid[:, :], -0.5, None, ALU.mult))
            step(nc.vector.tensor_scalar(half_gap[:, :], half_gap[:, :], 0.5, None, ALU.mult))
            step(nc.vector.tensor_scalar(times[:, :], times[:, :], 1.0, None, ALU.add))
            settle()
            step(nc.vector.tensor_scalar(chunk_f[:, :], half_gap[:, :], -1.0, None, ALU.mult))
            settle()
            step(nc.vector.tensor_tensor(half_gap[:, :], half_gap[:, :], chunk_f[:, :], ALU.max))
            settle()
            dve.wait_ge(degs_ready, NC)
            step(nc.vector.tensor_tensor(deg_in[:, :], deg_in2[:, :, 0], deg_in2[:, :, 1], ALU.add))
            settle()
            step(nc.vector.tensor_tensor(cnt[:, :], deg_in[:, :], deg_out[:, :], ALU.add))
            step(nc.vector.tensor_scalar(deg_in[:, :], deg_in[:, :], 1.0, None, ALU.add))
            settle()
            nc.vector.reciprocal(dinv[:, :], deg_in[:, :])
            for c in range(NC):
                cb = nc.vector.tensor_scalar(cb3[:, c, :], b3_all[:, :], cnt[:, c:c + 1], None, ALU.mult)
            cb.then_inc(cb3_ready, 1)

            def low_edges(g, b):
                dve.wait_ge(e_cast, g + 1)
                nc.vector.tensor_tensor(e_hl[ED:P, b, :], e_raw[ED:P, b, :], e_hl[ED:P, b, :].bitcast(F32),
                                        ALU.subtract).then_inc(e_ready, 1)

            def add_gathered(g, b, q, n):
                dve.wait_ge(z1_psum, 2 * g + q + 1)
                for t in range(2):
                    dve.wait_ge(gb_done[b][2 * q + t], 16 * (n + 1))
                wait(dve, z1t_psum, 2 * g + q - 1)
                nc.vector.tensor_tensor(z1_sb[:, q, :, :].rearrange("p t n -> p (t n)"), z1_bank[q][:, :],
                                        g_sb[:, b, 2 * q:2 * q + 2, :].rearrange("p t n -> p (t n)"),
                                        ALU.add).then_inc(z1_ready, 1)

            def low_pair(g, b, q):
                dve.wait_ge(h1_hi_ready, 2 * g + q + 1)
                part = slice(q * 2 * P, (q + 1) * 2 * P)
                nc.vector.scalar_tensor_tensor(h1_lo[:, b, :, part], z1t_bank[:, :].rearrange("p (k e) -> p k e", k=KH),
                                               0.0, h1_hi[:, b, :, part].bitcast(F32), ALU.max,
                                               ALU.subtract).then_inc(h1_lo_ready, 1)

            def low_messages(g, b):
                dve.wait_ge(m_hi_ready, g + 1)
                nc.vector.tensor_tensor(m_lo[:, b, :, :].rearrange("p t d -> p (t d)"), msg_bank[:, :],
                                        m_hi[:, b, :, :].rearrange("p t d -> p (t d)").bitcast(F32),
                                        ALU.subtract).then_inc(m_lo_ready, 1)

            def incidence(g, t):
                dve.wait_ge(dist_ready, GT * g + (t + 1))
                wait(dve, scattered, GT * g + (t - 3))
                tile = bass.ds(g * GT + t, 1)
                nc.vector.tensor_scalar(inc[:, t, :], dist[:, t, :], half_gap[:, tile], times[:, tile],
                                        ALU.is_equal, ALU.mult).then_inc(inc_ready, 1)

            def group(g, b, i):
                now, nxt, ahead, past = exists(g), exists(g + 1), exists(g + 2), exists(g - 1)
                if past:
                    incidence(g - 1, 2)
                    incidence(g - 1, 3)
                if nxt:
                    low_pair(g + 1, 1 - b, 0)
                if now:
                    incidence(g, 0)
                if nxt:
                    low_pair(g + 1, 1 - b, 1)
                if exists(g + 3):
                    low_edges(g + 3, 1 - b)
                if ahead:
                    add_gathered(g + 2, b, 0, i + 1)
                if now:
                    incidence(g, 1)
                if ahead:
                    add_gathered(g + 2, b, 1, i + 1)
                if now:
                    low_messages(g, b)

            run_groups(dve, group)

            for k in range(KH * NH):
                m, n = k // NH, k % NH
                dve.wait_ge(u1_psum, k + 1)
                nc.vector.tensor_tensor(uh_sb[:, m, n * HB:(n + 1) * HB], bank[2 + k][:, :],
                                        uh_sb[:, m, n * HB:(n + 1) * HB], ALU.add).then_inc(u1_added, 1)
            dve.wait_ge(u3_psum, NC)
            for k in range(NH):
                step(nc.vector.tensor_tensor(x1_sb[:, 4 * k:4 * k + 4, :].rearrange("p c d -> p (c d)"),
                                             bank[2 + k][:, :],
                                             xb_sb[:, 4 * k:4 * k + 4, :].rearrange("p c d -> p (c d)"), ALU.add))
            settle()
            layer_norm(x1_sb, var2_ready, std2_ready, h2n_ready)
            dve.wait_ge(sqrt_ready, 1)
            for c in range(NC):
                dve.wait_ge(xw_psum, NC)
                nc.vector.tensor_scalar(y_sb[:, c, :], bank[6 + c // 4][:, (c % 4) * D:(c % 4 + 1) * D],
                                        dinv[:, c:c + 1], None, ALU.mult).then_inc(y_ready, 1)
            dve.wait_ge(y_ready, NC)
            for half in range(NH):
                c0, c1 = half * NC // NH, (half + 1) * NC // NH
                dve.wait_ge(agg_psum, c1)
                step(nc.vector.tensor_tensor(o_sb[:, c0:c1, :].rearrange("p c d -> p (c d)"), bank[half][:, :],
                                             y_sb[:, c0:c1, :].rearrange("p c d -> p (c d)"), ALU.add))
                settle()
                for c in range(c0, c1):
                    nc.vector.scalar_tensor_tensor(o_sb[:, c, :], o_sb[:, c, :], dinv[:, c:c + 1], gb_all[:, :],
                                                   ALU.mult, ALU.add).then_inc(pre_ready, 1)
            for half in range(NH):
                c0, c1 = half * NC // NH, (half + 1) * NC // NH
                dve.wait_ge(gelu_ready, half + 1)
                nc.vector.tensor_tensor(o_sb[:, c0:c1, :], o_sb[:, c0:c1, :], x1_sb[:, c0:c1, :],
                                        ALU.add).then_inc(out_ready, 1)


def kernel(**inputs):
    import numpy as np
    import concourse.bacc as bacc
    from concourse.bass_utils import run_bass_kernel_spmd

    a = {k: np.asarray(v) for k, v in inputs.items()}
    tiles = a["src"].shape[0] // P

    def columns(v, n):
        return np.ascontiguousarray(v.reshape(-1, n).T)

    def row(v):
        return np.ascontiguousarray(v.reshape(1, -1))

    L = "L0_gnn_"
    arrays = {
        "x": a["x"],
        "src_cols": columns(a["src"], P),
        "dst_cols": columns(a["dst"], P),
        "edge_attr_t": np.ascontiguousarray(a["edge_attr_64"].T),
        "mW1": a[L + "mW1"], "mb1": row(a[L + "mb1"]),
        "mW2": a[L + "mW2"], "mb2_cols": columns(a[L + "mb2"], P),
        "mW3": a[L + "mW3"], "mb3": a[L + "mb3"],
        "uW1": a[L + "uW1"], "ub1_cols": columns(a[L + "ub1"], P),
        "uW2": a[L + "uW2"], "ub2_cols": columns(a[L + "ub2"], P),
        "uW3": a[L + "uW3"], "ub3": a[L + "ub3"],
        "gcn_W": a["L1_gnn_W"], "gcn_b": a["L1_gnn_b"],
    }
    arrays = {k: np.ascontiguousarray(v) for k, v in arrays.items()}
    nc = bacc.Bacc("TRN2", target_bir_lowering=False, num_devices=1)
    args = [nc.dram_tensor(k, list(v.shape), mybir.dt.from_np(v.dtype), kind="ExternalInput").ap()
            for k, v in arrays.items()]
    out = nc.dram_tensor("out", list(a["x"].shape), F32, kind="ExternalOutput").ap()
    gnn_preln_kernel(nc, *args, out)
    r = run_bass_kernel_spmd(nc, [arrays], core_ids=[0])
    return r.results[0]["out"]
```

```python
from contextlib import ExitStack

import concourse.bass as bass
from concourse import mybir

P = 128
ALU = mybir.AluOpType
ACT = mybir.ActivationFunctionType
F32 = mybir.dt.float32
F32R = mybir.dt.float32r
BF16 = mybir.dt.bfloat16
F16 = mybir.dt.float16
I32 = mybir.dt.int32
AX_X = mybir.AxisListType.X
LN_EPS = 1e-5


def gnn_preln_kernel(nc, x, src_cols, dst_cols, edge_attr_t, mW1, mb1, mW2, mb2_cols, mW3, mb3,
                     uW1, ub1_cols, uW2, ub2_cols, uW3, ub3, gcn_W, gcn_b, out):
    N, D = x.shape
    TILES = src_cols.shape[1]
    ED = edge_attr_t.shape[0]
    H = mW2.shape[0]
    NC = N // P
    KH = H // P
    GT = 4
    GE = GT * P
    GROUPS = TILES // GT
    HB = 512
    NH = N // HB
    HC = NC // NH
    halves_by_m = [(n, m) for n in range(NH) for m in range(KH)]
    VT = 12
    GRAIN = 2
    GRAINS = TILES // GRAIN
    RING = 2
    SLOTS = 6
    AT = 10
    PAIR_ATT = 32
    assert D == P and 2 * ED == P and H == 2 * P and GROUPS % 2 == 0

    table_a = nc.dram_tensor("table_a", [N, H], F32).ap()
    table_b = nc.dram_tensor("table_b", [N, H], F32).ap()

    with ExitStack() as ctx:
        def sb(name, shape, dt=F32):
            return ctx.enter_context(nc.sbuf_tensor(name, shape, dt))

        def sem(name):
            return ctx.enter_context(nc.semaphore(name))

        bank = [ctx.enter_context(nc.psum_tensor(f"bank{i}", [P, HB], F32)) for i in range(8)]
        acc_bank = bank[0:2]
        z1_bank = bank[4:6]
        z1t_bank = bank[2]
        z2_bank = [bank[3], bank[6]]
        msg_bank = bank[7]

        tab_bank = [bank[2], bank[3], bank[0], bank[1]]
        u1_bank = [bank[2:4], bank[4:6]]
        u2_bank = [bank[6:8], bank[0:2]]
        u3_bank = bank[2:4]
        h2t_bank = bank[4:6]
        xw_bank = bank[6:8]
        agg_bank = bank[0:4]

        x_sb = sb("x_sb", [P, NC, D])
        ends_i = sb("ends_i", [P, 2, TILES], I32)
        src_i, dst_i = ends_i[:, 0, :], ends_i[:, 1, :]
        w1_sb = sb("w1_sb", [P, 2, H])
        w1e_sb = sb("w1e_sb", [P, H])
        b1_row = sb("b1_row", [1, H])
        w2_sb = sb("w2_sb", [P, KH, H])
        b2_sb = sb("b2_sb", [P, KH])
        w3_sb = sb("w3_sb", [P, KH, D])
        b3_all = sb("b3_all", [P, D])
        u1_sb = sb("u1_sb", [P, 3, H])
        ub1_sb = sb("ub1_sb", [P, KH])
        u2_sb = sb("u2_sb", [P, KH, H])
        ub2_sb = sb("ub2_sb", [P, KH])
        u3_sb = sb("u3_sb", [P, KH, D])
        ub3_all = sb("ub3_all", [P, D])
        gw_sb = sb("gw_sb", [P, D])
        gb_all = sb("gb_all", [P, D])

        iota_h = sb("iota_h", [P, N], F16)
        ident = sb("ident", [P, P])
        ones_bf = sb("ones_bf", [P, P], BF16)
        zeros_bf = sb("zeros_bf", [P, HB], BF16)
        ones_row = sb("ones_row", [1, P])
        ones_col = sb("ones_col", [P, 1])

        w1e_hi = sb("w1e_hi", [P, H], F32R)
        w1e_lo = sb("w1e_lo", [P, H], F32R)
        w2_hi = sb("w2_hi", [P, KH, H], F32R)
        w2_lo = sb("w2_lo", [P, KH, H], F32R)
        b1_hi = sb("b1_hi", [1, H], F32R)
        b1_lo = sb("b1_lo", [1, H], F32R)
        one_r = sb("one_r", [1, P], F32R)
        u_node = sb("u_node", [P, 2, H])
        u_node_hi = sb("u_node_hi", [P, 2, H], F32R)
        u_node_lo = sb("u_node_lo", [P, 2, H], F32R)

        stats = sb("stats", [P, NC, 6])
        mv = sb("mv", [P, NC, 2])
        root = sb("root", [P, 2, NC])
        inv_root = sb("inv_root", [P, 2, NC])
        rstd, dinv = inv_root[:, 0, :], inv_root[:, 1, :]
        h_sb = sb("h_sb", [P, NC, D])
        tab_sb = sb("tab_sb", [P, NC, 2, H])
        uh_sb = sb("uh_sb", [P, KH, N])

        src_f = sb("src_f", [P, TILES + VT])
        dst_f = sb("dst_f", [P, TILES + VT])
        neg_dst = sb("neg_dst", [P, TILES + VT])
        neg_mid = sb("neg_mid", [P, TILES])
        half_gap = sb("half_gap", [P, TILES])
        times = sb("times", [P, TILES])
        chunk_i = sb("chunk_i", [P, TILES], I32)
        chunk_f = sb("chunk_f", [P, TILES])
        back_iota = sb("back_iota", [1, GRAINS])
        hi_f = sb("hi_f", [1, NC])
        lo_f = sb("lo_f", [1, NC])
        len_f = sb("len_f", [1, NC])
        cum_f = sb("cum_f", [1, NC + 1])
        range_i = sb("range_i", [1, NC, 3], I32)

        oh_src_c = sb("oh_src_c", [P, SLOTS, N], BF16)
        oh_dst_c = sb("oh_dst_c", [P, RING, VT, P], BF16)
        off_dst = sb("off_dst", [P, AT, P], F16)
        c_sb = sb("c_sb", [P, 2, N])
        ct_sb = sb("ct_sb", [P, NC, N])
        deg_in2 = sb("deg_in2", [P, NC, NH])
        deg_out2 = sb("deg_out2", [P, 2, NC])
        deg_out = sb("deg_out", [P, NC])
        deg_in = sb("deg_in", [P, NC])
        cnt = sb("cnt", [P, NC])
        cb3 = sb("cb3", [P, NC, D])

        gidx = sb("gidx", [P, 4, 2, 2], I32)
        g_sb = sb("g_sb", [P, 2, GT, H])
        e_raw = sb("e_raw", [P, 2, GE])
        e_hl = sb("e_hl", [P, 2, GE], F32R)
        z1_sb = sb("z1_sb", [P, 2, 2, H])
        h1_hi = sb("h1_hi", [P, 2, KH, GE], F32R)
        h1_lo = sb("h1_lo", [P, 2, KH, GE], F32R)
        h2_sb = sb("h2_sb", [P, KH, GE])
        m_hi = sb("m_hi", [P, 2, GT, D], F32R)
        m_lo = sb("m_lo", [P, 2, GT, D], F32R)
        inc = sb("inc", [P, GT, N], F32R)

        dist = oh_src_c[:, 0:GT, :].rearrange("p t n -> p (t n)").bitcast(F16).rearrange("p (t n) -> p t n", t=GT)
        ends_here = h2_sb[0:1, :, :].rearrange("p k n -> p (k n)").rearrange("p (c g) -> p c g", c=NC)
        in_chunk = g_sb[:, 0, :, :].rearrange("p t n -> p (t n)").bitcast(BF16).rearrange("p (c t) -> p c t", c=NC)
        h_hi, h_lo = inc[:, 2, :], inc[:, 3, :]
        w1_hi, w1_lo = inc[:, 1, 0:2 * H], inc[:, 1, 2 * H:4 * H]
        chunk_sum = h_sb[:, :, :]
        iota_f = ct_sb[:, 0, :]
        xb_sb = x_sb
        h_t = cb3[:, :, :].rearrange("p c d -> p (c d)")
        tab_all = tab_sb[:, :, :, :].rearrange("p c t n -> p (c t n)")
        u_a = tab_all[:, 0:KH * N].rearrange("p (k n) -> p k n", k=KH)
        sum_t = tab_all[:, KH * N:KH * N + N]
        x1_sb = tab_all[:, KH * N + N:KH * N + 2 * N].rearrange("p (c d) -> p c d", c=NC)
        y_sb = c_sb[:, 0, :].rearrange("p (c d) -> p c d", c=NC)
        o_sb = c_sb[:, 1, :].rearrange("p (c d) -> p c d", c=NC)

        splits = [
            (w1_sb[:, :, :].rearrange("p k n -> p (k n)"), w1_hi, w1_lo),
            (b1_row[:, :], b1_hi[:, :], b1_lo[:, :]),
            (u_node[:, :, :], u_node_hi[:, :, :], u_node_lo[:, :, :]),
            (w1e_sb[:, :], w1e_hi[:, :], w1e_lo[:, :]),
            (w2_sb[:, :, :], w2_hi[:, :, :], w2_lo[:, :, :]),
        ]
        W1_SPLITS = 2

        ld_x = sem("ld_x")
        ld_idx = sem("ld_idx")
        ld_w1 = sem("ld_w1")
        ld_w = sem("ld_w")
        consts_pool = sem("consts_pool")
        pool_step = sem("pool_step")
        dve_step = sem("dve_step")
        var_ready = sem("var_ready")
        std_ready = sem("std_ready")
        h_ready = sem("h_ready")
        ht_psum = sem("ht_psum")
        h_hi_ready = sem("h_hi_ready")
        h_lo_ready = sem("h_lo_ready")
        w_hi_ready = sem("w_hi_ready")
        w_lo_ready = sem("w_lo_ready")
        xb_ready = sem("xb_ready")
        u_node_ready = sem("u_node_ready")
        tab_psum = sem("tab_psum")
        tab_ready = sem("tab_ready")
        tab_stored = sem("tab_stored")
        uh_psum = sem("uh_psum")
        uh_ready = sem("uh_ready")
        chunks_marked = sem("chunks_marked")
        marks_psum = sem("marks_psum")
        ranges_ready = sem("ranges_ready")
        ends_ready = sem("ends_ready")
        mids_ready = sem("mids_ready")
        c_hot_dve = sem("c_hot_dve")
        c_hot_act = sem("c_hot_act")
        off_made = sem("off_made")
        c_used = sem("c_used")
        c_psum = sem("c_psum")
        c_ready = sem("c_ready")
        ct_psum = sem("ct_psum")
        ct_ready = sem("ct_ready")
        starts_counted = sem("starts_counted")
        cb3_ready = sem("cb3_ready")
        gidx_ready = sem("gidx_ready")
        ga_done = [[sem(f"ga_done{b}_{j}") for j in range(GT)] for b in range(2)]
        gb_done = [[sem(f"gb_done{b}_{j}") for j in range(GT)] for b in range(2)]
        e_loaded = [sem("e_loaded0"), sem("e_loaded1")]
        e_cast = sem("e_cast")
        e_ready = sem("e_ready")
        z1_psum = sem("z1_psum")
        z1_ready = sem("z1_ready")
        z1t_psum = sem("z1t_psum")
        h1_hi_ready = sem("h1_hi_ready")
        h1_lo_ready = sem("h1_lo_ready")
        z2_psum = sem("z2_psum")
        h2_ready = sem("h2_ready")
        m_psum = sem("m_psum")
        m_hi_ready = sem("m_hi_ready")
        m_lo_ready = sem("m_lo_ready")
        dist_ready = sem("dist_ready")
        inc_ready = sem("inc_ready")
        scattered = sem("scattered")
        sum_ready = [sem("sum_ready0"), sem("sum_ready1")]
        u1_psum = sem("u1_psum")
        u1_added = sem("u1_added")
        u1_ready = sem("u1_ready")
        u2_psum = sem("u2_psum")
        u2_ready = sem("u2_ready")
        u3_psum = sem("u3_psum")
        x1_ready = sem("x1_ready")
        var2_ready = sem("var2_ready")
        std2_ready = sem("std2_ready")
        h2n_ready = sem("h2n_ready")
        h2t_psum = sem("h2t_psum")
        h2t_ready = sem("h2t_ready")
        xw_psum = sem("xw_psum")
        y_ready = sem("y_ready")
        agg_psum = sem("agg_psum")
        pre_ready = sem("pre_ready")
        gelu_ready = sem("gelu_ready")
        out_ready = sem("out_ready")
        stored = sem("stored")

        block = ctx.enter_context(nc.Block())

        def exists(g):
            return not isinstance(g, int) or 0 <= g < GROUPS

        def wait(engine, semaphore, value):
            if not isinstance(value, int) or value > 0:
                engine.wait_ge(semaphore, value)

        UNUSED = VT * (RING - 1)

        MAX_VISITS = NC * -(-TILES // VT)

        def end_of_visits(engine, c):
            return engine.value_load(range_i[0:1, c, 0:1], min_val=1, max_val=MAX_VISITS)

        def visits(engine, c):
            end = end_of_visits(engine, c)
            shift = engine.value_load(range_i[0:1, c, 1:2], min_val=-VT * MAX_VISITS, max_val=TILES)

            def tile0_of(visit):
                return nc.s_assert_within(
                    visit * VT + shift, 0, TILES - GRAIN,
                    skip_runtime_bounds_check_because="visits of a chunk run over its range of tiles")
            return end, tile0_of

        LAST_CHUNKS = 2
        FIRST = -3

        def is_first(g):
            return isinstance(g, int) and g == 0

        def run_groups(engine, group, start, after=None):
            for g in range(start, 2):
                group(g, g % 2, g // 2)
                if after and g in after:
                    after[g]()
            with engine.Fori(1, GROUPS // 2 - 2) as i:
                for b in range(2):
                    group(2 * i + b, b, i)
            for g in range(GROUPS - 4, GROUPS + 1):
                group(g, g % 2, g // 2)

        @block.sync
        def _(sp):
            sp.dma_start(x_sb[:, :, :], x.rearrange("(c p) d -> p c d", p=P)).then_inc(ld_x, 16)
            sp.dma_start(dst_i, dst_cols).then_inc(ld_idx, 16)
            sp.dma_start(src_i, src_cols).then_inc(ld_idx, 16)
            sp.dma_start(w1_sb[:, :, :], mW1[0:2 * D, :].rearrange("(k p) n -> p k n", p=P)).then_inc(ld_w1, 16)
            sp.dma_start(b1_row[:, :], mb1).then_inc(ld_w1, 16)
            loads = [
                (w1e_sb[0:ED, :], mW1[2 * D:2 * D + ED, :]),
                (w1e_sb[ED:P, :], mW1[2 * D:2 * D + ED, :]),
                (u1_sb[:, :, :], uW1.rearrange("(k p) n -> p k n", p=P)),
                (ub1_sb[:, :], ub1_cols),
                (w2_sb[:, :, :], mW2.rearrange("(k p) n -> p k n", p=P)),
                (b2_sb[:, :], mb2_cols),
                (w3_sb[:, :, :], mW3.rearrange("(k p) n -> p k n", p=P)),
                (b3_all[:, :], mb3.partition_broadcast(P)),
                (u2_sb[:, :, :], uW2.rearrange("(k p) n -> p k n", p=P)),
                (ub2_sb[:, :], ub2_cols),
                (u3_sb[:, :, :], uW3.rearrange("(k p) n -> p k n", p=P)),
                (ub3_all[:, :], ub3.partition_broadcast(P)),
                (gw_sb[:, :], gcn_W),
                (gb_all[:, :], gcn_b.partition_broadcast(P)),
            ]
            for to, frm in loads:
                sp.dma_start(to, frm).then_inc(ld_w, 16)

            def load_edges(g, b):
                cols = edge_attr_t[:, bass.ds(g * GE, GE)]
                sp.dma_start(e_raw[0:ED, b, :], cols).then_inc(e_loaded[b], 16)
                sp.dma_start(e_raw[ED:P, b, :], cols).then_inc(e_loaded[b], 16)

            load_edges(0, 0)
            load_edges(1, 1)
            sp.wait_ge(tab_ready, NC)
            sp.dma_start(table_a.rearrange("(c p) n -> p c n", p=P), tab_sb[:, :, 0, :]).then_inc(tab_stored, 16)
            sp.dma_start(table_b.rearrange("(c p) n -> p c n", p=P), tab_sb[:, :, 1, :]).then_inc(tab_stored, 16)
            with sp.Fori(0, GROUPS // 2 - 1) as i:
                for b in range(2):
                    sp.wait_ge(e_ready, 2 * i + b + 1)
                    load_edges(2 * i + b + 2, b)
            for pair in range(NC // 2):
                sp.wait_ge(out_ready, pair + 1)
                rows = slice(2 * pair * P, 2 * (pair + 1) * P)
                sp.dma_start(out[rows, :].rearrange("(c p) d -> p c d", p=P),
                             o_sb[:, 2 * pair:2 * pair + 2, :]).then_inc(stored, 16)
            sp.wait_ge(stored, 16 * NC // 2)

        @block.gpsimd
        def _(pool):
            steps = [0]

            def step(ins):
                steps[0] += 1
                ins.then_inc(pool_step, 1)
                pool.wait_ge(pool_step, steps[0])

            nc.gpsimd.iota(iota_f[:, :], pattern=[[1, N]], base=0, channel_multiplier=0,
                           allow_small_or_imprecise_dtypes=True).then_inc(consts_pool, 1)
            nc.gpsimd.memset(ones_bf[:, :], 1.0).then_inc(consts_pool, 1)
            nc.gpsimd.memset(zeros_bf[:, :], 0.0).then_inc(consts_pool, 1)
            nc.gpsimd.memset(ones_row[:, :], 1.0).then_inc(consts_pool, 1)
            nc.gpsimd.memset(ones_col[:, :], 1.0).then_inc(consts_pool, 1)
            nc.gpsimd.iota(back_iota[:, :], pattern=[[-1, GRAINS]], base=GRAINS, channel_multiplier=0,
                           allow_small_or_imprecise_dtypes=True).then_inc(consts_pool, 1)
            step(nc.gpsimd.memset(ident[:, :], 0.0))
            nc.gpsimd.affine_select(out=ident[:, :], in_=ident[:, :], compare_op=ALU.not_equal, fill=1.0,
                                    base=0, pattern=[[-1, P]], channel_multiplier=1).then_inc(consts_pool, 1)
            for k, (whole, hi, lo) in enumerate(splits):
                if k == W1_SPLITS:
                    pool.wait_ge(ld_w, 16 * 14)
                    nc.gpsimd.tensor_tensor(u_node[:, 0, :], u1_sb[:, 0, :], u1_sb[:, 2, :],
                                            ALU.add).then_inc(u_node_ready, 1)
                pool.wait_ge(w_hi_ready, k + 1)
                nc.gpsimd.tensor_tensor(lo, whole, hi.bitcast(F32), ALU.subtract).then_inc(w_lo_ready, 1)
            pool.wait_ge(ld_idx, 32)

            def gather_src(p, s, n):
                b, q = s // 2, s % 2
                wait(pool, z1_ready, p - 3)
                copied = p + 1
                if not isinstance(p, int):
                    copied = pool.to_reg(copied)
                nc.gpsimd.tensor_copy(gidx[:, s, :, :], ends_i[:, :, bass.ds(p * 2, 2)]).then_inc(gidx_ready, 1)
                pool.wait_ge(tab_stored, 32)
                pool.wait_ge(gidx_ready, copied)
                for t in range(2):
                    j = 2 * q + t
                    nc.gpsimd.indirect_dma_start(
                        g_sb[:, b, j, :], None, table_a,
                        bass.IndirectOffsetOnAxis(ap=gidx[:, s, 0, t:t + 1], axis=0),
                    ).then_inc(ga_done[b][j], 16)

            def gather_dst(p, s, n):
                b, q = s // 2, s % 2
                landed = 16 * (n + 1)
                if not isinstance(p, int):
                    landed = pool.to_reg(landed)
                for t in range(2):
                    j = 2 * q + t
                    pool.wait_ge(tab_stored, 32)
                    pool.wait_ge(ga_done[b][j], landed)
                    nc.gpsimd.indirect_dma_start(
                        g_sb[:, b, j, :], None, table_b,
                        bass.IndirectOffsetOnAxis(ap=gidx[:, s, 1, t:t + 1], axis=0), compute_op=ALU.add,
                    ).then_inc(gb_done[b][j], 16)

            def gather_step(p, s, n):
                if not isinstance(p, int) or p + 1 < 2 * GROUPS:
                    gather_src(p + 1, (s + 1) % 4, n + (s + 1) // 4)
                gather_dst(p, s, n)

            gather_src(0, 0, 0)
            for s in range(3):
                gather_step(s, s, 0)
            gather_dst(3, 3, 0)
            for c in range(1, NC - LAST_CHUNKS):
                pool.wait_ge(ct_ready, c + 1)
                before = ct_sb[:, :, 0:P] if c == 1 else chunk_sum
                wait(pool, starts_counted, c - 1)
                nc.gpsimd.tensor_tensor(chunk_sum, before, ct_sb[:, :, c * P:(c + 1) * P],
                                        ALU.add).then_inc(starts_counted, 1)
                if c == NC // 2:
                    gather_src(4, 0, 1)
                    gather_step(4, 0, 1)
            for s in range(1, 4):
                gather_step(4 + s, s, 1)
            with pool.Fori(2, GROUPS // 2 - 1) as i:
                for s in range(4):
                    gather_step(4 * i + s, s, i)
            for s in range(4):
                gather_step(2 * GROUPS - 4 + s, s, GROUPS // 2 - 1)
            nc.gpsimd.tensor_tensor(xb_sb[:, :, :], x_sb[:, :, :],
                                    ub3_all[:, :].unsqueeze(1).broadcast_to([P, NC, D]), ALU.add).then_inc(xb_ready, 1)

        @block.tensor
        def _(pe):
            pe.wait_ge(consts_pool, 7)
            for c in range(NC):
                if c % HC == 0:
                    pe.wait_ge(h_ready, c // HC + 1)
                mm = nc.tensor.transpose(bank[c // HC][:, (c % HC) * P:(c % HC + 1) * P], h_sb[:, c, :], ident[:, :])
                if c % HC == HC - 1:
                    mm.then_inc(ht_psum, 1)
            pe.wait_ge(w_lo_ready, W1_SPLITS)
            for c in range(NC):
                if c == 0 or c == 3:
                    pe.wait_ge(h_lo_ready, 1 if c == 0 else 2)
                if c >= 4:
                    pe.wait_ge(tab_ready, c - 3)
                if c == 2:
                    pe.wait_ge(chunks_marked, 1)
                    marks = in_chunk.rearrange("p c (g t) -> p t (c g)", t=GRAIN)
                    for q in range(NH):
                        for t in range(GRAIN):
                            mm = nc.tensor.matmul(bank[4 + q][0:1, :], ones_bf[:, 0:1], marks[:, t, q * HB:(q + 1) * HB],
                                                  start=(t == 0), stop=(t == GRAIN - 1))
                    mm.then_inc(marks_psum, 1)
                to = tab_bank[c % 4][:, :]
                part = slice(c * P, (c + 1) * P)
                nc.tensor.matmul(to, h_hi[:, part], w1_hi[:, :], start=True, stop=False, skip_group_check=True)
                nc.tensor.matmul(to, h_hi[:, part], w1_lo[:, :], start=False, stop=False, skip_group_check=True)
                nc.tensor.matmul(to, h_lo[:, part], w1_hi[:, :], start=False, stop=False, skip_group_check=True)
                nc.tensor.matmul(to[:, 0:H], one_r[:, :], b1_hi[:, :], start=False, stop=False, skip_group_check=True)
                nc.tensor.matmul(to[:, 0:H], one_r[:, :], b1_lo[:, :], start=False, stop=True,
                                 skip_group_check=True).then_inc(tab_psum, 1)
            def update_of_node(k):
                m, n = k // NH, k % NH
                if k == 0:
                    pe.wait_ge(w_lo_ready, len(splits))
                    pe.wait_ge(tab_ready, NC)
                if k >= 2:
                    pe.wait_ge(uh_ready, k - 1)
                to = bank[k % 2][:, :]
                pairs = [x.rearrange("p (b a n) -> p b a n", a=2, n=PAIR_ATT)
                         for x in (to, h_hi[:, n * HB:(n + 1) * HB], h_lo[:, n * HB:(n + 1) * HB])]
                part = slice(m * P, (m + 1) * P)
                for j, (w, x) in enumerate(((u_node_hi, h_hi), (u_node_lo, h_hi), (u_node_hi, h_lo))):
                    nc.tensor.matmul(to, w[:, 0, part], x[:, n * HB:(n + 1) * HB], start=(j == 0), stop=False,
                                     skip_group_check=True)
                for w, x in ((u_node_hi, 1), (u_node_lo, 1), (u_node_hi, 2)):
                    for a in range(2):
                        mm = nc.tensor.matmul(pairs[0][:, :, a, :], w[:, 1, part], pairs[x][:, :, 1 - a, :],
                                              start=False, stop=(w is u_node_hi and x == 2), skip_group_check=True)
                mm.then_inc(uh_psum, 1)

            for k in range(KH * NH):
                update_of_node(k)

            def first_layer(g, b, q):
                if q == 0:
                    pe.wait_ge(e_ready, g + 1)
                for t in range(2):
                    ee = e_hl[:, b, (2 * q + t) * P:(2 * q + t + 1) * P]
                    to = z1_bank[q][:, t * H:(t + 1) * H]
                    nc.tensor.matmul(to, ee, w1e_hi[:, :], start=(t == 0), stop=False, skip_group_check=True)
                    mm = nc.tensor.matmul(to, ee, w1e_lo[:, :], start=False, stop=True, skip_group_check=True)
                mm.then_inc(z1_psum, 1)

            def transpose_pair(g, q):
                wait(pe, z1_ready, 2 * g + q + 1)
                wait(pe, h1_lo_ready, 2 * g + q)
                for k in range(KH):
                    for t in range(2):
                        mm = nc.tensor.transpose(z1t_bank[:, (2 * k + t) * P:(2 * k + t + 1) * P],
                                                 z1_sb[:, q, t, k * P:(k + 1) * P], ident[:, :])
                mm.then_inc(z1t_psum, 1)

            def second_layer(g, b, m):
                if m == 0:
                    pe.wait_ge(h1_lo_ready, 2 * g + 2)
                wait(pe, h2_ready, 2 * g + m - 1)
                parts = [(w, a, k) for w, a in ((w2_hi, h1_hi), (w2_lo, h1_hi), (w2_hi, h1_lo)) for k in range(KH)]
                for n, (w, a, k) in enumerate(parts):
                    mm = nc.tensor.matmul(z2_bank[m][:, :], w[:, k, m * P:(m + 1) * P], a[:, b, k, :],
                                          start=(n == 0), stop=(n == len(parts) - 1))
                mm.then_inc(z2_psum, 1)

            def messages(g, tiles):
                if tiles[0] == 0:
                    pe.wait_ge(h2_ready, 2 * g + 2)
                    wait(pe, m_lo_ready, g)
                for t in tiles:
                    for k in range(KH):
                        mm = nc.tensor.matmul(msg_bank[:, t * D:(t + 1) * D], h2_sb[:, k, t * P:(t + 1) * P],
                                              w3_sb[:, k, :], start=(t == 0 and k == 0), stop=(k == KH - 1),
                                              skip_group_check=True)
                mm.then_inc(m_psum, 1)

            def scatter(g, b, t):
                if t == 0:
                    pe.wait_ge(m_lo_ready, g + 1)
                pe.wait_ge(inc_ready, GT * g + (t + 1))
                for part in (m_hi, m_lo):
                    for n in range(NH):
                        mm = nc.tensor.matmul(acc_bank[n][:, :], part[:, b, t, :], inc[:, t, n * HB:(n + 1) * HB],
                                              start=False, stop=False, skip_group_check=True)
                mm.then_inc(scattered, 1)

            def start_sums():
                pe.wait_ge(cb3_ready, 1)
                for c in range(NC):
                    nc.tensor.matmul(acc_bank[c // 4][:, (c % 4) * P:(c % 4 + 1) * P], cb3[:, c, :], ident[:, :],
                                     start=(c % 4 == 0), stop=False, skip_group_check=True)

            def group(g, b, i):
                now, nxt, ahead, past = exists(g), exists(g + 1), exists(g + 2), exists(g - 1)
                if now:
                    second_layer(g, b, 0)
                if nxt:
                    transpose_pair(g + 1, 0)
                if now:
                    second_layer(g, b, 1)
                if is_first(g - 1):
                    start_sums()
                if past:
                    scatter(g - 1, 1 - b, 0)
                if is_first(g + 1):
                    turn_chunk(NC - 1)
                if nxt:
                    transpose_pair(g + 1, 1)
                if past:
                    scatter(g - 1, 1 - b, 1)
                if now:
                    messages(g, (0, 1))
                if ahead:
                    first_layer(g + 2, b, 0)
                if now:
                    messages(g, (2, 3))
                if ahead:
                    first_layer(g + 2, b, 1)
                if past:
                    scatter(g - 1, 1 - b, 2)
                    scatter(g - 1, 1 - b, 3)

            pe.wait_ge(ranges_ready, 1)
            for g in (FIRST, FIRST + 1):
                group(g, g % 2, g // 2)
            pe.wait_ge(uh_ready, KH * NH)

            def turn_chunk(c):
                pe.wait_ge(c_ready, c + 1)
                wait(pe, ct_ready, c)
                for s in range(NC):
                    mm = nc.tensor.transpose(bank[6 + s // 4][:, (s % 4) * P:(s % 4 + 1) * P],
                                             c_sb[:, c % 2, s * P:(s + 1) * P], ident[:, :])
                mm.then_inc(ct_psum, 1)

            start = 0
            for c in range(NC):
                end = end_of_visits(pe, c)
                cb = bank[2 * (c % 2):2 * (c % 2) + 2]
                if c >= 2:
                    pe.wait_ge(c_ready, c - 1)
                for n in range(NH):
                    nc.tensor.matmul(cb[n][:, :], zeros_bf[:, 0:P], zeros_bf[:, :], start=True, stop=False,
                                     skip_group_check=True)
                with pe.Fori(start, end) as visit:
                    for j in range(VT):
                        if j == 0 or j == AT // 2:
                            pe.wait_ge(c_hot_act, visit * 2 + (3 if j == 0 else 4))
                        pe.wait_ge(c_hot_dve, visit * VT + (j + 1))
                        for n in range(NH):
                            mm = nc.tensor.matmul(cb[n][:, :], oh_dst_c[:, visit % RING, j, :],
                                                  oh_src_c[:, j % SLOTS, n * HB:(n + 1) * HB],
                                                  start=False, stop=False, skip_group_check=True)
                        mm.then_inc(c_used, 1)
                for n in range(NH):
                    mm = nc.tensor.matmul(cb[n][:, 0:2], zeros_bf[:, 0:P], zeros_bf[:, 0:2], start=False, stop=True,
                                          skip_group_check=True)
                mm.then_inc(c_psum, 1)
                start = end
                if c:
                    turn_chunk(c - 1)
            pe.wait_ge(c_ready, NC)

            def before_second_layer():
                pe.wait_ge(ct_ready, NC)

            run_groups(pe, group, FIRST + 2, {-1: before_second_layer})

            for n, m in halves_by_m:
                if m == 0:
                    pe.wait_ge(sum_ready[n], 1)
                nc.tensor.matmul(u1_bank[n][m][:, :], u1_sb[:, 1, m * P:(m + 1) * P], sum_t[:, n * HB:(n + 1) * HB],
                                 start=True, stop=True).then_inc(u1_psum, 1)

            def update_second(n, m):
                if m == 0:
                    pe.wait_ge(u1_ready, KH * (n + 1))
                for kk in range(KH):
                    mm = nc.tensor.matmul(u2_bank[n][m][:, :], u2_sb[:, kk, m * P:(m + 1) * P],
                                          uh_sb[:, kk, n * HB:(n + 1) * HB], start=(kk == 0), stop=(kk == KH - 1))
                mm.then_inc(u2_psum, 1)

            def update_third(n):
                pe.wait_ge(u2_ready, KH * (n + 1))
                for c in range(n * HC, (n + 1) * HC):
                    for kk in range(KH):
                        mm = nc.tensor.matmul(u3_bank[n][:, (c % HC) * D:(c % HC + 1) * D],
                                              u_a[:, kk, c * P:(c + 1) * P], u3_sb[:, kk, :],
                                              start=(kk == 0 and c % HC == 0), stop=(kk == KH - 1), skip_group_check=True)
                mm.then_inc(u3_psum, 1)

            update_second(0, 0)
            update_second(0, 1)
            update_second(1, 0)
            update_third(0)
            update_second(1, 1)
            update_third(1)

            def turn_h(n):
                pe.wait_ge(h2n_ready, n + 1)
                for c in range(n * HC, (n + 1) * HC):
                    mm = nc.tensor.transpose(h2t_bank[n][:, (c % HC) * P:(c % HC + 1) * P], h_sb[:, c, :], ident[:, :])
                mm.then_inc(h2t_psum, 1)

            def times_w(n):
                pe.wait_ge(h2t_ready, n + 1)
                for c in range(n * HC, (n + 1) * HC):
                    mm = nc.tensor.matmul(xw_bank[n][:, (c % HC) * D:(c % HC + 1) * D], h_t[:, c * P:(c + 1) * P],
                                          gw_sb[:, :], start=(c % HC == 0), stop=True, skip_group_check=True)
                mm.then_inc(xw_psum, 1)

            def aggregate(n, chunks):
                pe.wait_ge(y_ready, n + 1)
                for c in chunks:
                    for s in range(n * HC, (n + 1) * HC):
                        mm = nc.tensor.matmul(agg_bank[c // 2][:, (c % 2) * D:(c % 2 + 1) * D],
                                              ct_sb[:, s, c * P:(c + 1) * P], y_sb[:, s, :],
                                              start=(s == 0 and c % 2 == 0), stop=(s == NC - 1), skip_group_check=True)
                    if n == NH - 1:
                        mm.then_inc(agg_psum, 1)

            turn_h(0)
            times_w(0)
            aggregate(0, range(2))
            turn_h(1)
            aggregate(0, range(2, NC - 2))
            times_w(1)
            aggregate(0, range(NC - 2, NC))
            aggregate(1, range(NC))

        @block.scalar
        def _(act):
            act.wait_ge(ld_w1, 32)
            for whole, hi, lo in splits[0:W1_SPLITS]:
                nc.scalar.copy(hi, whole).then_inc(w_hi_ready, 1)
            act.wait_ge(consts_pool, 7)
            nc.scalar.copy(one_r[:, :], ones_row[:, :])
            act.wait_ge(var_ready, 1)
            nc.scalar.activation(root[:, 0, :], root[:, 0, :], ACT.Sqrt).then_inc(std_ready, 1)
            for n in range(NH):
                act.wait_ge(ht_psum, n + 1)
                nc.scalar.activation(h_hi[:, n * HB:(n + 1) * HB], bank[n][:, :], ACT.Relu).then_inc(h_hi_ready, 1)
            act.wait_ge(ld_w, 16 * 14)
            nc.scalar.activation(u_node[:, 1, :], u1_sb[:, 2, :], ACT.Copy, scale=-1.0).then_inc(u_node_ready, 1)
            for k, (whole, hi, lo) in enumerate(splits):
                if k >= W1_SPLITS:
                    if k == W1_SPLITS:
                        act.wait_ge(u_node_ready, 2)
                    nc.scalar.copy(hi, whole).then_inc(w_hi_ready, 1)

            def split_edges(g, b, n):
                act.wait_ge(e_loaded[b], 32 * (n + 1))
                wait(act, z1_psum, 2 * (g - 1))
                nc.scalar.copy(e_hl[:, b, :], e_raw[:, b, :]).then_inc(e_cast, 1)

            def relu_pair(g, b, q):
                act.wait_ge(z1t_psum, 2 * g + q + 1)
                wait(act, z2_psum, 2 * g - 2)
                nc.scalar.activation(h1_hi[:, b, :, q * 2 * P:(q + 1) * 2 * P],
                                     z1t_bank[:, :].rearrange("p (k e) -> p k e", k=KH), ACT.Relu).then_inc(h1_hi_ready, 1)

            def relu_second(g, m):
                act.wait_ge(z2_psum, 2 * g + m + 1)
                wait(act, m_psum, 2 * g)
                nc.scalar.activation(h2_sb[:, m, :], z2_bank[m][:, :], ACT.Relu, bias=b2_sb[:, m:m + 1]).then_inc(h2_ready, 1)

            def distance(g, t):
                wait(act, inc_ready, GT * g + (t - 3))
                nc.scalar.activation(dist[:, t, :], iota_h[:, :], ACT.Abs,
                                     bias=neg_mid[:, bass.ds(g * GT + t, 1)]).then_inc(dist_ready, 1)

            def high_messages(g, b):
                act.wait_ge(m_psum, 2 * g + 2)
                wait(act, scattered, GT * (g - 1))
                nc.scalar.copy(m_hi[:, b, :, :].rearrange("p t d -> p (t d)"), msg_bank[:, :]).then_inc(m_hi_ready, 1)

            def group(g, b, i):
                now, nxt = exists(g), exists(g + 1)
                if now:
                    relu_second(g, 0)
                if nxt:
                    relu_pair(g + 1, 1 - b, 0)
                if now:
                    relu_second(g, 1)
                    distance(g, 1)
                if is_first(g + 1):
                    transpose_out(NC - 1)
                if nxt:
                    relu_pair(g + 1, 1 - b, 1)
                if exists(g + 3):
                    split_edges(g + 3, 1 - b, i + 1 + b)
                if now:
                    distance(g, 2)
                    high_messages(g, b)
                    distance(g, 3)
                if nxt:
                    distance(g + 1, 0)

            for g in (FIRST, FIRST + 1):
                group(g, g % 2, g // 2)

            for c in range(NC):
                act.wait_ge(tab_psum, c + 1)
                nc.scalar.copy(tab_sb[:, c, :, :].rearrange("p t n -> p (t n)"), tab_bank[c % 4][:, :]).then_inc(tab_ready, 1)
            for k in range(KH * NH):
                m, n = k // NH, k % NH
                act.wait_ge(uh_psum, k + 1)
                nc.scalar.activation(uh_sb[:, m, n * HB:(n + 1) * HB], bank[k % 2][:, :], ACT.Identity,
                                     bias=ub1_sb[:, m:m + 1]).then_inc(uh_ready, 1)
            def chunk_rows(c, start):
                end, tile0_of = visits(act, c)
                with act.Fori(start, end) as visit:
                    tile0 = tile0_of(visit)
                    for half in range(2):
                        tiles = range(half * AT // 2, (half + 1) * AT // 2)
                        act.wait_ge(c_hot_act, visit * 2 + (half + 1))
                        for j in tiles:
                            nc.scalar.activation(off_dst[:, j, :], iota_h[:, c * P:(c + 1) * P], ACT.Abs,
                                                 bias=neg_dst[:, bass.ds(tile0 + j, 1)]).then_inc(off_made, 1)
                        act.wait_ge(off_made, visit * AT + tiles[-1] + 1)
                        if half == 0:
                            act.wait_ge(c_used, visit * VT + 1)
                        part = slice(tiles[0], tiles[-1] + 1)
                        nc.scalar.activation(oh_dst_c[:, visit % RING, part, :], off_dst[:, part, :], ACT.Relu,
                                             bias=ones_col[:, :], scale=-1.0).then_inc(c_hot_act, 1)
                return end

            def counts_out(c):
                act.wait_ge(c_psum, c + 1)
                wait(act, ct_psum, c - 1)
                for n in range(NH):
                    cp = nc.scalar.activation(c_sb[:, c % 2, n * HB:(n + 1) * HB], bank[2 * (c % 2) + n][:, :],
                                              ACT.Copy, accum_out=deg_in2[:, c, n:n + 1])
                cp.then_inc(c_ready, 1)

            def transpose_out(c):
                act.wait_ge(ct_psum, c + 1)
                for n in range(NH):
                    cp = nc.scalar.copy(ct_sb[:, 4 * n:4 * n + 4, c * P:(c + 1) * P],
                                        bank[6 + n][:, :].rearrange("p (s d) -> p s d", s=4))
                cp.then_inc(ct_ready, 1)

            nc.scalar.copy(off_dst[:, 0, 0:1], ones_col[:, :]).then_inc(c_hot_act, 2)
            act.wait_ge(ranges_ready, 1)
            start = 0
            for c in range(NC):
                start = chunk_rows(c, start)
                if c >= 2:
                    transpose_out(c - 2)
                if c >= 1:
                    counts_out(c - 1)
            counts_out(NC - 1)
            transpose_out(NC - 2)

            act.wait_ge(mids_ready, 1)
            run_groups(act, group, FIRST + 2)

            act.wait_ge(scattered, GT * GROUPS)
            nc.scalar.copy(sum_t[:, 0:HB], acc_bank[0][:, :]).then_inc(sum_ready[0], 1)
            for k, (n, m) in enumerate(halves_by_m):
                act.wait_ge(u1_added, k + 1)
                nc.scalar.activation(uh_sb[:, m, n * HB:(n + 1) * HB], uh_sb[:, m, n * HB:(n + 1) * HB],
                                     ACT.Relu).then_inc(u1_ready, 1)
            for k, (n, m) in enumerate(halves_by_m):
                act.wait_ge(u2_psum, k + 1)
                nc.scalar.activation(u_a[:, m, n * HB:(n + 1) * HB], u2_bank[n][m][:, :], ACT.Relu,
                                     bias=ub2_sb[:, m:m + 1]).then_inc(u2_ready, 1)
            for n in range(NH):
                half = slice(n * HC, (n + 1) * HC)
                act.wait_ge(var2_ready, n + 1)
                nc.scalar.activation(root[:, :, half], root[:, :, half], ACT.Sqrt).then_inc(std2_ready, 1)
                act.wait_ge(h2t_psum, n + 1)
                nc.scalar.activation(h_t[:, n * HB:(n + 1) * HB], h2t_bank[n][:, :], ACT.Relu).then_inc(h2t_ready, 1)
            for pair in range(NC // 2):
                part = slice(2 * pair, 2 * pair + 2)
                act.wait_ge(pre_ready, pair + 1)
                nc.scalar.activation(o_sb[:, part, :], o_sb[:, part, :], ACT.Gelu).then_inc(gelu_ready, 1)

        @block.vector
        def _(dve):
            steps = [0]

            def step(ins):
                steps[0] += 1
                ins.then_inc(dve_step, 1)

            def settle():
                dve.wait_ge(dve_step, steps[0])

            def row_stats(rows, chunks, ready):
                for c in chunks:
                    step(nc.vector.bn_stats(stats[:, c, :], rows[:, c, :]))
                settle()
                for c in chunks:
                    step(nc.vector.bn_aggr(mv[:, c, :], stats[:, c, :]))
                settle()
                part = slice(chunks[0], chunks[-1] + 1)
                nc.vector.tensor_scalar(root[:, 0, part], mv[:, part, 1], LN_EPS, None, ALU.add).then_inc(ready, 1)

            def normalise(rows, chunks, roots, final):
                part = slice(chunks[0], chunks[-1] + 1)
                step(nc.vector.reciprocal(inv_root[:, 0:roots, part], root[:, 0:roots, part]))
                settle()
                for c in chunks:
                    hh = nc.vector.tensor_scalar(h_sb[:, c, :], rows[:, c, :], mv[:, c, 0:1], rstd[:, c:c + 1],
                                                 ALU.subtract, ALU.mult)
                hh.then_inc(final, 1)

            dve.wait_ge(consts_pool, 7)
            step(nc.vector.tensor_copy(iota_h[:, :], iota_f[:, :]))
            for to, none in ((src_f, -1.0), (dst_f, -1.0), (neg_dst, 1.0)):
                nc.vector.memset(to[:, TILES:TILES + VT], none).then_inc(ends_ready, 1)
            dve.wait_ge(ld_idx, 32)
            step(nc.vector.tensor_scalar(chunk_i[:, :], dst_i, 7, None, ALU.arith_shift_right))
            nc.vector.tensor_copy(src_f[:, 0:TILES], src_i).then_inc(ends_ready, 1)
            nc.vector.tensor_copy(dst_f[:, 0:TILES], dst_i).then_inc(ends_ready, 1)
            nc.vector.tensor_scalar(neg_dst[:, 0:TILES], dst_i, -1.0, None, ALU.mult).then_inc(ends_ready, 1)
            settle()
            step(nc.vector.tensor_copy(chunk_f[:, :], chunk_i[:, :]))
            settle()
            dve.wait_ge(ld_x, 16)
            row_stats(x_sb, range(NC), var_ready)
            dve.wait_ge(std_ready, 1)
            for n in range(NH):
                normalise(x_sb, range(n * HC, (n + 1) * HC), 1, h_ready)
            for n in range(NH):
                part = slice(n * HB, (n + 1) * HB)
                dve.wait_ge(h_hi_ready, n + 1)
                nc.vector.scalar_tensor_tensor(h_lo[:, part], bank[n][:, :], 0.0, h_hi[:, part].bitcast(F32),
                                               ALU.max, ALU.subtract).then_inc(h_lo_ready, 1)
            for c in range(NC):
                mark = nc.vector.tensor_scalar(in_chunk[:, c, :], chunk_f[:, :], float(c), None, ALU.is_equal)
            mark.then_inc(chunks_marked, 1)
            def low_edges(g, b):
                dve.wait_ge(e_cast, g + 1)
                nc.vector.tensor_tensor(e_hl[ED:P, b, :], e_raw[ED:P, b, :], e_hl[ED:P, b, :].bitcast(F32),
                                        ALU.subtract).then_inc(e_ready, 1)

            def add_gathered(g, b, q, n):
                dve.wait_ge(z1_psum, 2 * g + q + 1)
                for t in range(2):
                    dve.wait_ge(gb_done[b][2 * q + t], 16 * (n + 1))
                wait(dve, z1t_psum, 2 * g + q - 1)
                nc.vector.tensor_tensor(z1_sb[:, q, :, :].rearrange("p t n -> p (t n)"), z1_bank[q][:, :],
                                        g_sb[:, b, 2 * q:2 * q + 2, :].rearrange("p t n -> p (t n)"),
                                        ALU.add).then_inc(z1_ready, 1)

            def low_pair(g, b, q):
                dve.wait_ge(h1_hi_ready, 2 * g + q + 1)
                part = slice(q * 2 * P, (q + 1) * 2 * P)
                nc.vector.scalar_tensor_tensor(h1_lo[:, b, :, part], z1t_bank[:, :].rearrange("p (k e) -> p k e", k=KH),
                                               0.0, h1_hi[:, b, :, part].bitcast(F32), ALU.max,
                                               ALU.subtract).then_inc(h1_lo_ready, 1)

            def low_messages(g, b):
                dve.wait_ge(m_hi_ready, g + 1)
                nc.vector.tensor_tensor(m_lo[:, b, :, :].rearrange("p t d -> p (t d)"), msg_bank[:, :],
                                        m_hi[:, b, :, :].rearrange("p t d -> p (t d)").bitcast(F32),
                                        ALU.subtract).then_inc(m_lo_ready, 1)

            def incidence(g, t):
                dve.wait_ge(dist_ready, GT * g + (t + 1))
                wait(dve, scattered, GT * g + (t - 3))
                tile = bass.ds(g * GT + t, 1)
                nc.vector.tensor_scalar(inc[:, t, :], dist[:, t, :], half_gap[:, tile], times[:, tile],
                                        ALU.is_equal, ALU.mult).then_inc(inc_ready, 1)

            def group(g, b, i):
                now, nxt, ahead, past = exists(g), exists(g + 1), exists(g + 2), exists(g - 1)
                if past:
                    incidence(g - 1, 2)
                    incidence(g - 1, 3)
                if nxt:
                    low_pair(g + 1, 1 - b, 0)
                if now:
                    incidence(g, 0)
                if nxt:
                    low_pair(g + 1, 1 - b, 1)
                if exists(g + 3):
                    low_edges(g + 3, 1 - b)
                if is_first(g):
                    bias_of_sums()
                if ahead:
                    add_gathered(g + 2, b, 0, i + 1)
                if now:
                    incidence(g, 1)
                if ahead:
                    add_gathered(g + 2, b, 1, i + 1)
                if now:
                    low_messages(g, b)

            group(FIRST, FIRST % 2, FIRST // 2)
            dve.wait_ge(marks_psum, 1)
            for weights, to in ((back_iota[:, :], lo_f), (iota_f[0:1, 1:GRAINS + 1], hi_f)):
                for q in range(NH):
                    chunks = slice(q * HC, (q + 1) * HC)
                    step(nc.vector.scalar_tensor_tensor(
                        ends_here[:, chunks, :], bank[4 + q][0:1, :].rearrange("p (c g) -> p c g", c=HC), 0.0,
                        weights.unsqueeze(1).broadcast_to([1, HC, GRAINS]), ALU.is_gt, ALU.mult))
                settle()
                step(nc.vector.tensor_reduce(to[:, :], ends_here[:, :, :], AX_X, ALU.max))
                settle()
            step(nc.vector.tensor_scalar(hi_f[:, :], hi_f[:, :], 1.0, None, ALU.max))
            step(nc.vector.tensor_scalar(lo_f[:, :], lo_f[:, :], -1.0, float(GRAINS), ALU.mult, ALU.add))
            settle()
            step(nc.vector.tensor_scalar(len_f[:, :], hi_f[:, :], -1.0, None, ALU.add))
            settle()
            step(nc.vector.tensor_tensor(lo_f[:, :], lo_f[:, :], len_f[:, :], ALU.min))
            settle()
            VG = VT // GRAIN
            step(nc.vector.tensor_tensor(len_f[:, :], hi_f[:, :], lo_f[:, :], ALU.subtract))
            settle()
            starts = iota_f[0:1, 0:GRAINS:VG]
            passes = ends_here[:, :, 0:starts.shape[1]]
            step(nc.vector.tensor_tensor(passes, len_f[:, :].unsqueeze(2).broadcast_to(list(passes.shape)),
                                         starts.unsqueeze(1).broadcast_to(list(passes.shape)), ALU.is_gt))
            settle()
            step(nc.vector.tensor_reduce(len_f[:, :], passes, AX_X, ALU.add))
            step(nc.vector.memset(cum_f[:, 0:1], 0.0))
            settle()
            for c in range(NC):
                step(nc.vector.tensor_tensor(cum_f[:, c + 1:c + 2], cum_f[:, c:c + 1], len_f[:, c:c + 1], ALU.add))
                settle()
            step(nc.vector.tensor_scalar(hi_f[:, :], cum_f[:, 0:NC], -float(VG), None, ALU.mult))
            settle()
            step(nc.vector.tensor_tensor(lo_f[:, :], lo_f[:, :], hi_f[:, :], ALU.add))
            settle()
            step(nc.vector.tensor_copy(range_i[:, :, 0], cum_f[:, 1:NC + 1]))
            step(nc.vector.tensor_scalar(range_i[:, :, 1], lo_f[:, :], float(GRAIN), None, ALU.mult))
            settle()
            dve.wait_ge(ends_ready, 6)
            def middles():
                step(nc.vector.tensor_tensor(neg_mid[:, :], src_f[:, 0:TILES], dst_f[:, 0:TILES], ALU.add))
                step(nc.vector.tensor_tensor(half_gap[:, :], src_f[:, 0:TILES], dst_f[:, 0:TILES], ALU.subtract))
                step(nc.vector.tensor_tensor(times[:, :], src_f[:, 0:TILES], dst_f[:, 0:TILES], ALU.is_equal))
                settle()
                step(nc.vector.tensor_scalar(neg_mid[:, :], neg_mid[:, :], -0.5, None, ALU.mult))
                step(nc.vector.tensor_scalar(half_gap[:, :], half_gap[:, :], 0.5, None, ALU.mult))
                step(nc.vector.tensor_scalar(times[:, :], times[:, :], 1.0, None, ALU.add))
                settle()
                step(nc.vector.tensor_scalar(chunk_f[:, :], half_gap[:, :], -1.0, None, ALU.mult))
                settle()
                nc.vector.tensor_tensor(half_gap[:, :], half_gap[:, :], chunk_f[:, :], ALU.max).then_inc(mids_ready, 1)
                dve.wait_ge(mids_ready, 1)

            def starts_of_first_chunks():
                dve.wait_ge(starts_counted, NC - 1 - LAST_CHUNKS)
                step(nc.vector.tensor_reduce(deg_out2[:, 0, :], chunk_sum, AX_X, ALU.add))

            def starts_of_last_chunks():
                dve.wait_ge(ct_ready, NC)
                step(nc.vector.tensor_reduce(deg_out2[:, 1, :], ct_sb[:, :, (NC - LAST_CHUNKS) * P:N], AX_X, ALU.add))
                step(nc.vector.tensor_tensor(deg_in[:, :], deg_in2[:, :, 0], deg_in2[:, :, 1], ALU.add))
                settle()
                step(nc.vector.tensor_scalar(root[:, 1, :], deg_in[:, :], 1.0, None, ALU.add))
                step(nc.vector.tensor_tensor(deg_out[:, :], deg_out2[:, 0, :], deg_out2[:, 1, :], ALU.add))

            def bias_of_sums():
                settle()
                step(nc.vector.tensor_tensor(cnt[:, :], deg_in[:, :], deg_out[:, :], ALU.add))
                settle()
                nc.vector.tensor_tensor(cb3[:, :, :], b3_all[:, :].unsqueeze(1).broadcast_to([P, NC, D]),
                                        cnt[:, :].unsqueeze(2).broadcast_to([P, NC, D]), ALU.mult).then_inc(cb3_ready, 1)

            nc.vector.memset(cnt[:, :], 0.0).then_inc(c_used, UNUSED)
            nc.vector.tensor_copy(range_i[:, :, 2], cum_f[:, 1:NC + 1]).then_inc(ranges_ready, 1)
            dve.wait_ge(ranges_ready, 1)
            middles()
            start = 0
            for c in range(NC):
                if c == 2:
                    group(FIRST + 1, (FIRST + 1) % 2, (FIRST + 1) // 2)
                end, tile0_of = visits(dve, c)
                with dve.Fori(start, end) as visit:
                    tile0 = tile0_of(visit)
                    dve.wait_ge(c_used, visit * VT + 1)
                    for j in range(AT, VT):
                        nc.vector.tensor_scalar(oh_dst_c[:, visit % RING, j, :], iota_h[:, c * P:(c + 1) * P],
                                                dst_f[:, bass.ds(tile0 + j, 1)], None, ALU.is_equal)
                    for j in range(VT):
                        dve.wait_ge(c_used, visit * VT + (UNUSED - SLOTS + j + 1))
                        nc.vector.tensor_scalar(oh_src_c[:, j % SLOTS, :], iota_h[:, :],
                                                src_f[:, bass.ds(tile0 + j, 1)], None,
                                                ALU.is_equal).then_inc(c_hot_dve, 1)
                start = end
            starts_of_first_chunks()
            run_groups(dve, group, FIRST + 2, {-1: starts_of_last_chunks})

            dve.wait_ge(scattered, GT * GROUPS)
            nc.vector.tensor_copy(sum_t[:, HB:N], acc_bank[1][:, :]).then_inc(sum_ready[1], 1)
            for k, (n, m) in enumerate(halves_by_m):
                dve.wait_ge(u1_psum, k + 1)
                nc.vector.tensor_tensor(uh_sb[:, m, n * HB:(n + 1) * HB], u1_bank[n][m][:, :],
                                        uh_sb[:, m, n * HB:(n + 1) * HB], ALU.add).then_inc(u1_added, 1)

            chunks_of = [range(n * HC, (n + 1) * HC) for n in range(NH)]

            def residual(n):
                half = slice(n * HC, (n + 1) * HC)
                dve.wait_ge(u3_psum, n + 1)
                step(nc.vector.tensor_tensor(x1_sb[:, half, :].rearrange("p c d -> p (c d)"), u3_bank[n][:, :],
                                             xb_sb[:, half, :].rearrange("p c d -> p (c d)"), ALU.add))

            dve.wait_ge(xb_ready, 1)
            def scaled_by_root(n):
                dve.wait_ge(xw_psum, n + 1)
                for c in chunks_of[n]:
                    yy = nc.vector.tensor_scalar(y_sb[:, c, :], xw_bank[n][:, (c % HC) * D:(c % HC + 1) * D],
                                                 dinv[:, c:c + 1], None, ALU.mult)
                yy.then_inc(y_ready, 1)

            for n in range(NH):
                residual(n)
                settle()
                row_stats(x1_sb, chunks_of[n], var2_ready)
                if n == NH - 1:
                    scaled_by_root(0)
                dve.wait_ge(std2_ready, n + 1)
                normalise(x1_sb, chunks_of[n], 2, h2n_ready)
            scaled_by_root(NH - 1)
            dve.wait_ge(y_ready, NH)
            for c in range(NC):
                step(nc.vector.scalar_tensor_tensor(o_sb[:, c, :], y_sb[:, c, :], dinv[:, c:c + 1], gb_all[:, :],
                                                    ALU.mult, ALU.add))
            settle()

            def before_gelu(pair):
                dve.wait_ge(agg_psum, 2 * (pair + 1))
                for c in (2 * pair, 2 * pair + 1):
                    pre = nc.vector.scalar_tensor_tensor(o_sb[:, c, :], agg_bank[pair][:, (c % 2) * D:(c % 2 + 1) * D],
                                                         dinv[:, c:c + 1], o_sb[:, c, :], ALU.mult, ALU.add)
                pre.then_inc(pre_ready, 1)

            def after_gelu(pair):
                part = slice(2 * pair, 2 * pair + 2)
                dve.wait_ge(gelu_ready, pair + 1)
                nc.vector.tensor_tensor(o_sb[:, part, :], o_sb[:, part, :], x1_sb[:, part, :],
                                        ALU.add).then_inc(out_ready, 1)

            for pair in range(NC // 2):
                before_gelu(pair)
                if pair:
                    after_gelu(pair - 1)
            after_gelu(NC // 2 - 1)


def kernel(**inputs):
    import numpy as np
    import concourse.bacc as bacc
    from concourse.bass_utils import run_bass_kernel_spmd

    a = {k: np.asarray(v) for k, v in inputs.items()}
    tiles = a["src"].shape[0] // P

    def columns(v, n):
        return np.ascontiguousarray(v.reshape(-1, n).T)

    def row(v):
        return np.ascontiguousarray(v.reshape(1, -1))

    L = "L0_gnn_"
    arrays = {
        "x": a["x"],
        "src_cols": columns(a["src"], P),
        "dst_cols": columns(a["dst"], P),
        "edge_attr_t": np.ascontiguousarray(a["edge_attr_64"].T),
        "mW1": a[L + "mW1"], "mb1": row(a[L + "mb1"]),
        "mW2": a[L + "mW2"], "mb2_cols": columns(a[L + "mb2"], P),
        "mW3": a[L + "mW3"], "mb3": a[L + "mb3"],
        "uW1": a[L + "uW1"], "ub1_cols": columns(a[L + "ub1"], P),
        "uW2": a[L + "uW2"], "ub2_cols": columns(a[L + "ub2"], P),
        "uW3": a[L + "uW3"], "ub3": a[L + "ub3"],
        "gcn_W": a["L1_gnn_W"], "gcn_b": a["L1_gnn_b"],
    }
    arrays = {k: np.ascontiguousarray(v) for k, v in arrays.items()}
    nc = bacc.Bacc("TRN2", target_bir_lowering=False, num_devices=1)
    args = [nc.dram_tensor(k, list(v.shape), mybir.dt.from_np(v.dtype), kind="ExternalInput").ap()
            for k, v in arrays.items()]
    out = nc.dram_tensor("out", list(a["x"].shape), F32, kind="ExternalOutput").ap()
    gnn_preln_kernel(nc, *args, out)
    r = run_bass_kernel_spmd(nc, [arrays], core_ids=[0])
    return r.results[0]["out"]
```
